# Optimizing a Trainium2 kernel written in Bass

```python
import numpy as np
import jax
import jax.numpy as jnp

def _softmax(x, axis=-1):
    return jax.nn.softmax(x, axis=axis)

def _gelu(x):
    return jax.nn.gelu(x, approximate=True)

def _silu(x):
    return jax.nn.silu(x)

def _sigmoid(x):
    return jax.nn.sigmoid(x)

def _layernorm(x, axis=-1, eps=1e-05):
    m = jnp.mean(x, axis=axis, keepdims=True)
    v = jnp.var(x, axis=axis, keepdims=True)
    return (x - m) / jnp.sqrt(v + eps)

def _scatter_add(tgt, idx, src, axis=0):
    return tgt.at[idx].add(src)

def _segment_sum(src, seg, n):
    return jax.ops.segment_sum(src, seg, n)
kernel_name = 'mk_macaron_d1_jaxref_r8_9af496'

def setup_inputs(seed: int=0):
    np.random.seed(seed)
    _w = jnp.asarray

    def _L0_attn_setup():
        import jax, jax.numpy as jnp
        import numpy as np
        LN_EPS = 1e-05

        def _forward(x, W_in, conv_w, conv_b, a_param, W_out, ln_w, ln_b):
            B, T, D = x.shape
            K = conv_w.shape[-1]
            proj = jnp.einsum('btd,ed->bte', x, W_in)
            gate, val = (proj[..., :D], proj[..., D:])
            g = jax.nn.sigmoid(gate)
            v = jax.lax.conv_general_dilated(val.transpose(0, 2, 1), conv_w, window_strides=(1,), padding=[(K // 2, K // 2)], feature_group_count=D, dimension_numbers=('NCH', 'OIH', 'NCH'))
            v = (v + conv_b[None, :, None]).transpose(0, 2, 1)
            a = jnp.tanh(a_param)
            gv = g * v

            def step(h, u):
                h = a * h + u
                return (h, h)
            h0 = jnp.zeros((B, D), dtype=x.dtype)
            _, y = jax.lax.scan(step, h0, gv.transpose(1, 0, 2))
            y = y.transpose(1, 0, 2)
            res = x + jnp.einsum('btd,ed->bte', y, W_out)
            mu = jnp.mean(res, axis=-1, keepdims=True)
            var = jnp.mean(jnp.square(res - mu), axis=-1, keepdims=True)
            return (res - mu) * jax.lax.rsqrt(var + LN_EPS) * ln_w + ln_b
        key = jax.random.key(seed)
        ks = jax.random.split(key, 6)
        B, T, D, K = (8, 256, 128, 5)
        x = jax.random.normal(ks[0], (B, T, D), dtype=jnp.float32)
        W_in = jax.random.normal(ks[1], (2 * D, D), dtype=jnp.float32) * (1.0 / np.sqrt(D))
        conv_w = jax.random.normal(ks[2], (D, 1, K), dtype=jnp.float32) * (1.0 / np.sqrt(K))
        conv_b = jax.random.normal(ks[3], (D,), dtype=jnp.float32) * 0.1
        a_param = jax.random.normal(ks[4], (D,), dtype=jnp.float32)
        W_out = jax.random.normal(ks[5], (D, D), dtype=jnp.float32) * (1.0 / np.sqrt(D))
        ln_w = jnp.ones((D,), dtype=jnp.float32)
        ln_b = jnp.zeros((D,), dtype=jnp.float32)
        return {'x': x, 'W_in': W_in, 'conv_w': conv_w, 'conv_b': conv_b, 'a_param': a_param, 'W_out': W_out, 'ln_w': ln_w, 'ln_b': ln_b}
    _L0_attn_in = _L0_attn_setup()

    def _L0_ffn_setup():
        import jax, jax.numpy as jnp
        import numpy as np
        from jax import lax
        B, S, H = (2, 128, 128)
        I = 64
        E = 32
        TOP_K = 4
        N_GROUP = 4
        TOPK_GROUP = 2
        SCALE = 2.5
        N_SHARED = 2
        SH_I = I * N_SHARED

        def _route(tokens, router_weight, router_bias):
            logits = tokens.astype(jnp.float32) @ router_weight.astype(jnp.float32).T
            scores = jax.nn.sigmoid(logits)
            sfc = scores + router_bias[None, :]
            T = tokens.shape[0]
            grp = sfc.reshape(T, N_GROUP, E // N_GROUP)
            group_scores = lax.top_k(grp, 2)[0].sum(-1)
            _, gidx = lax.top_k(group_scores, TOPK_GROUP)
            gmask = jax.nn.one_hot(gidx, N_GROUP, dtype=sfc.dtype).sum(1)
            smask = jnp.broadcast_to(gmask[:, :, None], (T, N_GROUP, E // N_GROUP)).reshape(T, E)
            tmp = jnp.where(smask > 0, sfc, 0.0)
            _, topk_idx = lax.top_k(tmp, TOP_K)
            topk_w = jnp.take_along_axis(scores, topk_idx, axis=1)
            topk_w = topk_w / (topk_w.sum(-1, keepdims=True) + 1e-20)
            topk_w = topk_w * SCALE
            return (topk_idx, topk_w)
        key = jax.random.key(seed)
        ks = jax.random.split(key, 10)
        std = 0.02
        return {'hidden_states': jax.random.normal(ks[0], (B, S, H), jnp.float32), 'router_weight': jax.random.normal(ks[1], (E, H), jnp.float32) * std, 'router_bias': jnp.zeros((E,), jnp.float32), 'gate_w': jax.random.normal(ks[2], (E, I, H), jnp.float32) * std, 'up_w': jax.random.normal(ks[3], (E, I, H), jnp.float32) * std, 'down_w': jax.random.normal(ks[4], (E, H, I), jnp.float32) * std, 'shared_gate_w': jax.random.normal(ks[5], (SH_I, H), jnp.float32) * std, 'shared_up_w': jax.random.normal(ks[6], (SH_I, H), jnp.float32) * std, 'shared_down_w': jax.random.normal(ks[7], (H, SH_I), jnp.float32) * std}
    _L0_ffn_in = _L0_ffn_setup()
    _d = {'L0_attn_x': _L0_attn_in['x'], 'L0_attn_W_in': _L0_attn_in['W_in'], 'L0_attn_conv_w': _L0_attn_in['conv_w'], 'L0_attn_conv_b': _L0_attn_in['conv_b'], 'L0_attn_a_param': _L0_attn_in['a_param'], 'L0_attn_W_out': _L0_attn_in['W_out'], 'L0_attn_ln_w': _L0_attn_in['ln_w'], 'L0_attn_ln_b': _L0_attn_in['ln_b'], 'L0_ffn_router_weight': _L0_ffn_in['router_weight'], 'L0_ffn_router_bias': _L0_ffn_in['router_bias'], 'L0_ffn_gate_w': _L0_ffn_in['gate_w'], 'L0_ffn_up_w': _L0_ffn_in['up_w'], 'L0_ffn_down_w': _L0_ffn_in['down_w'], 'L0_ffn_shared_gate_w': _L0_ffn_in['shared_gate_w'], 'L0_ffn_shared_up_w': _L0_ffn_in['shared_up_w'], 'L0_ffn_shared_down_w': _L0_ffn_in['shared_down_w']}
    _x0 = _d['L0_attn_x']
    _d['L0_attn_x'] = jax.random.normal(jax.random.fold_in(jax.random.key(seed), 1), (16, 256, 128), dtype=_x0.dtype)
    del _x0
    return _d

def reference(L0_attn_x, L0_attn_W_in, L0_attn_conv_w, L0_attn_conv_b, L0_attn_a_param, L0_attn_W_out, L0_attn_ln_w, L0_attn_ln_b, L0_ffn_router_weight, L0_ffn_router_bias, L0_ffn_gate_w, L0_ffn_up_w, L0_ffn_down_w, L0_ffn_shared_gate_w, L0_ffn_shared_up_w, L0_ffn_shared_down_w):

    def _L0_attn_ref(x, W_in, conv_w, conv_b, a_param, W_out, ln_w, ln_b):
        import jax, jax.numpy as jnp
        import numpy as np
        LN_EPS = 1e-05

        def _forward(x, W_in, conv_w, conv_b, a_param, W_out, ln_w, ln_b):
            B, T, D = x.shape
            K = conv_w.shape[-1]
            proj = jnp.einsum('btd,ed->bte', x, W_in)
            gate, val = (proj[..., :D], proj[..., D:])
            g = jax.nn.sigmoid(gate)
            v = jax.lax.conv_general_dilated(val.transpose(0, 2, 1), conv_w, window_strides=(1,), padding=[(K // 2, K // 2)], feature_group_count=D, dimension_numbers=('NCH', 'OIH', 'NCH'))
            v = (v + conv_b[None, :, None]).transpose(0, 2, 1)
            a = jnp.tanh(a_param)
            gv = g * v

            def step(h, u):
                h = a * h + u
                return (h, h)
            h0 = jnp.zeros((B, D), dtype=x.dtype)
            _, y = jax.lax.scan(step, h0, gv.transpose(1, 0, 2))
            y = y.transpose(1, 0, 2)
            res = x + jnp.einsum('btd,ed->bte', y, W_out)
            mu = jnp.mean(res, axis=-1, keepdims=True)
            var = jnp.mean(jnp.square(res - mu), axis=-1, keepdims=True)
            return (res - mu) * jax.lax.rsqrt(var + LN_EPS) * ln_w + ln_b
        return _forward(x, W_in, conv_w, conv_b, a_param, W_out, ln_w, ln_b)

    def _L0_ffn_ref(hidden_states, router_weight, router_bias, gate_w, up_w, down_w, shared_gate_w, shared_up_w, shared_down_w):
        import jax, jax.numpy as jnp
        import numpy as np
        from jax import lax
        B, S, H = (2, 128, 128)
        I = 64
        E = 32
        TOP_K = 4
        N_GROUP = 4
        TOPK_GROUP = 2
        SCALE = 2.5
        N_SHARED = 2
        SH_I = I * N_SHARED

        def _route(tokens, router_weight, router_bias):
            logits = tokens.astype(jnp.float32) @ router_weight.astype(jnp.float32).T
            scores = jax.nn.sigmoid(logits)
            sfc = scores + router_bias[None, :]
            T = tokens.shape[0]
            grp = sfc.reshape(T, N_GROUP, E // N_GROUP)
            group_scores = lax.top_k(grp, 2)[0].sum(-1)
            _, gidx = lax.top_k(group_scores, TOPK_GROUP)
            gmask = jax.nn.one_hot(gidx, N_GROUP, dtype=sfc.dtype).sum(1)
            smask = jnp.broadcast_to(gmask[:, :, None], (T, N_GROUP, E // N_GROUP)).reshape(T, E)
            tmp = jnp.where(smask > 0, sfc, 0.0)
            _, topk_idx = lax.top_k(tmp, TOP_K)
            topk_w = jnp.take_along_axis(scores, topk_idx, axis=1)
            topk_w = topk_w / (topk_w.sum(-1, keepdims=True) + 1e-20)
            topk_w = topk_w * SCALE
            return (topk_idx, topk_w)
        tokens = hidden_states.reshape(-1, H)
        topk_idx, topk_w = _route(tokens, router_weight, router_bias)
        gate_vals = jax.nn.silu(jnp.einsum('th,eih->tei', tokens, gate_w))
        up_vals = jnp.einsum('th,eih->tei', tokens, up_w)
        hidden_vals = gate_vals * up_vals
        expert_out = jnp.einsum('tei,ehi->teh', hidden_vals, down_w)
        sel = jnp.take_along_axis(expert_out, topk_idx[:, :, None], axis=1)
        mixed = (sel * topk_w[:, :, None].astype(sel.dtype)).sum(1)
        mixed = mixed.reshape(hidden_states.shape)
        sg = jax.nn.silu(jnp.einsum('bsh,ih->bsi', hidden_states, shared_gate_w))
        su = jnp.einsum('bsh,ih->bsi', hidden_states, shared_up_w)
        shared = jnp.einsum('bsi,hi->bsh', sg * su, shared_down_w)
        return mixed + shared
    x = L0_attn_x
    x = x + 0.5 * _L0_ffn_ref(_layernorm(x, axis=-1), L0_ffn_router_weight, L0_ffn_router_bias, L0_ffn_gate_w, L0_ffn_up_w, L0_ffn_down_w, L0_ffn_shared_gate_w, L0_ffn_shared_up_w, L0_ffn_shared_down_w)
    x = x + _L0_attn_ref(_layernorm(x, axis=-1), L0_attn_W_in, L0_attn_conv_w, L0_attn_conv_b, L0_attn_a_param, L0_attn_W_out, L0_attn_ln_w, L0_attn_ln_b)
    x = x + 0.5 * _L0_ffn_ref(_layernorm(x, axis=-1), L0_ffn_router_weight, L0_ffn_router_bias, L0_ffn_gate_w, L0_ffn_up_w, L0_ffn_down_w, L0_ffn_shared_gate_w, L0_ffn_shared_up_w, L0_ffn_shared_down_w)
    return x

_drawn_inputs = setup_inputs


def setup_inputs(seed=0):
    import zlib

    import numpy as np

    out = dict(_drawn_inputs(seed))
    spreads = {'L0_attn_ln_w': (1.0, 0.2), 'L0_attn_ln_b': (0.0, 0.1), 'L0_ffn_router_bias': (0.0, 0.8)}
    factors = {'L0_ffn_router_weight': 8.0,
     'L0_ffn_gate_w': 8.0,
     'L0_ffn_up_w': 8.0,
     'L0_ffn_down_w': 8.0,
     'L0_ffn_shared_gate_w': 8.0,
     'L0_ffn_shared_up_w': 8.0,
     'L0_ffn_shared_down_w': 8.0}
    for name, (base, spread) in spreads.items():
        noise = np.random.default_rng([zlib.crc32(name.encode()), seed]).standard_normal(out[name].shape)
        drawn = base * np.exp(spread * noise) if base else spread * noise
        out[name] = jnp.asarray(drawn.astype(out[name].dtype))
    for name, factor in factors.items():
        out[name] = (out[name] * factor).astype(out[name].dtype)
    return out
```

```python
from contextlib import ExitStack

import concourse.bass as bass
from concourse import mybir

F32 = mybir.dt.float32
F32R = mybir.dt.float32r
ALU = mybir.AluOpType
ACT = mybir.ActivationFunctionType
AX = mybir.AxisListType

P = 128
SEQS, SEQ = 16, 256
BLK = 512
NBLK = SEQS * SEQ // BLK
TT = BLK // P
SB = BLK // SEQ
E, I = 32, 64
NPAIR = E * I // P
NT = NPAIR + 1
NG, PG = 4, E // 4
GTOP, TOP = 2, 4
SCALE = 2.5
K = 5
PADK = K // 2
EPS = 1e-5
FAR, GONE = -2.0e38, -3.0e38
NBATCH = 14


def gate_tile(j):
    return 4 + 12 * (j // 4) + j % 4 if j < NPAIR else 52


def up_tile(j):
    return gate_tile(j) + (4 if j < NPAIR else 1)


def down_tile(j):
    return gate_tile(j) + (8 if j < NPAIR else 2)


WIN_G, WIN_V, WOUT, WROUTER = 0, 1, 2, 3


class Steps:

    def __init__(self, engine, sem, base):
        self.engine, self.sem, self.base, self.n = engine, sem, base, 0

    def done(self, instruction):
        instruction.then_inc(self.sem, 1)
        self.n += 1

    def wait(self):
        self.engine.wait_ge(self.sem, self.base + self.n)


def macaron_kernel(nc, x, W_in, conv_w, conv_b, a_param, W_out, ln_w, ln_b, router_w, router_b,
                   gate_w, up_w, down_w, sh_gate, sh_up, sh_down, out):
    x_blk = x.rearrange("a s d -> (a s) d").rearrange("(n t p) d -> n p t d", t=TT, p=P)
    out_blk = out.rearrange("a s d -> (a s) d").rearrange("(n t p) d -> n p t d", t=TT, p=P)

    with ExitStack() as ctx:
        def sb(name, shape, dt=F32):
            return ctx.enter_context(nc.sbuf_tensor(name, shape, dt))

        def psum(name):
            return ctx.enter_context(nc.psum_tensor(name, [P, BLK], F32))

        def sem(name):
            return ctx.enter_context(nc.semaphore(name))

        gate_ps = [psum("gate_ps0"), psum("gate_ps1")]
        up_ps = [psum("up_ps0"), psum("up_ps1")]
        wb_ps = [psum("wb_ps0"), psum("wb_ps1")]
        down_ps = psum("down_ps")
        side = psum("side")
        side_te = side[:, 0:TT * E].rearrange("p (t e) -> p t e", t=TT)
        side_td = side[:, :].rearrange("p (t d) -> p t d", t=TT)

        raw = sb("raw", [P, NBATCH * 4, P])
        wt_hi = sb("wt_hi", [P, NBATCH * 4, P], F32R)
        wt_lo = sb("wt_lo", [P, NBATCH * 4, P], F32R)
        ident = sb("ident", [P, P])
        zeros = sb("zeros", [P, NPAIR, P])
        pick_half = sb("pick_half", [P, NPAIR, P])
        pick = sb("pick", [P, NPAIR, P], F32R)
        neg_half = sb("neg_half", [P, TT])
        eps = sb("eps", [P, TT])
        hold = sb("hold", [P, 1])
        pool_hold = sb("pool_hold", [P, 1])
        beat_at = sb("beat_at", [P, NG, NG])
        bias_b = sb("bias_b", [P, E])
        lnw_b = sb("lnw_b", [P, P])
        lnb_b = sb("lnb_b", [P, P])
        taps = sb("taps", [P, K])
        taps_half = sb("taps_half", [P, K])
        cbias = sb("cbias", [P, 1])
        cbias_half = sb("cbias_half", [P, 1])
        a_raw = sb("a_raw", [P, 1])
        a_tanh = sb("a_tanh", [P, 1])
        ones = sb("ones", [P, BLK])
        decay = sb("decay", [P, BLK])
        silu_sb = [sb("silu_sb0", [P, BLK]), sb("silu_sb1", [P, BLK])]
        weighted = [sb("weighted0", [P, BLK]), sb("weighted1", [P, BLK])]
        hid = [sb("hid0", [P, BLK]), sb("hid1", [P, BLK])]
        hid_hi = [sb("hid_hi0", [P, BLK], F32R), sb("hid_hi1", [P, BLK], F32R)]
        hid_lo = [sb("hid_lo0", [P, BLK], F32R), sb("hid_lo1", [P, BLK], F32R)]
        LN = (1, 2, 3, 4)
        stats = {k: sb(f"stats{k}", [P, TT, 6]) for k in LN}
        meanvar = {k: sb(f"meanvar{k}", [P, TT, 2]) for k in LN}
        var_eps = {k: sb(f"var_eps{k}", [P, TT]) for k in LN}
        neg_mean = {k: sb(f"neg_mean{k}", [P, TT]) for k in LN}
        rstd = {k: sb(f"rstd{k}", [P, TT]) for k in LN}
        normed = {k: sb(f"normed{k}", [P, TT, P]) for k in LN}
        xT_hi = {k: sb(f"xT_hi{k}", [P, BLK], F32R) for k in (1, 2, 4)}
        xT_lo = {k: sb(f"xT_lo{k}", [P, BLK], F32R) for k in (1, 2, 4)}
        x_ln = sb("x_ln", [P, TT, P])
        x_res = sb("x_res", [P, TT, P])
        x1 = sb("x1", [P, TT, P])
        x1_b = sb("x1_b", [P, TT, P])
        x2 = sb("x2", [P, TT, P])
        x3 = sb("x3", [P, TT, P])
        ffn_sb = {k: sb(f"ffn_sb{k}", [P, BLK]) for k in (1, 4)}
        gate_t = sb("gate_t", [P, BLK])
        val_pad = sb("val_pad", [P, SB, SEQ + 2 * PADK])
        conv = [sb("conv0", [P, SB, SEQ]), sb("conv1", [P, SB, SEQ])]
        gated = sb("gated", [P, BLK])
        y = sb("y", [P, BLK])
        y_hi = sb("y_hi", [P, BLK], F32R)
        y_lo = sb("y_lo", [P, BLK], F32R)
        res = sb("res", [P, TT, P])
        scaled = sb("scaled", [P, TT, P])
        tiny = sb("tiny", [P, TT, E])
        logit = sb("logit", [P, TT, E])
        logit_silu = sb("logit_silu", [P, TT, E])
        logit_inv = sb("logit_inv", [P, TT, E])
        score = sb("score", [P, TT, E])
        biased = sb("biased", [P, TT, E])
        hi4 = sb("hi4", [P, TT * NG, 4])
        lo4 = sb("lo4", [P, TT * NG, 4])
        hi2 = sb("hi2", [P, TT * NG, 2])
        lo2a = sb("lo2a", [P, TT * NG, 2])
        lo2b = sb("lo2b", [P, TT * NG, 2])
        lo2 = sb("lo2", [P, TT * NG, 2])
        hi1 = sb("hi1", [P, TT * NG, 1])
        lo1a = sb("lo1a", [P, TT * NG, 1])
        lo1b = sb("lo1b", [P, TT * NG, 1])
        lo1 = sb("lo1", [P, TT * NG, 1])
        gsum = sb("gsum", [P, TT, NG])
        gdiff = sb("gdiff", [P, TT, NG * NG])
        beats = sb("beats", [P, TT * NG, NG])
        grank = sb("grank", [P, TT * NG])
        gmask = sb("gmask", [P, TT * NG])
        masked0 = sb("masked0", [P, TT, E])
        masked = sb("masked", [P, TT, E + TOP])
        top8 = sb("top8", [P, TT, 8])
        replaced = sb("replaced", [P, TT, E + TOP])
        chosen = sb("chosen", [P, TT, E])
        wsum = sb("wsum", [P, TT])
        wsum_e = sb("wsum_e", [P, TT])
        winv = sb("winv", [P, TT])
        weight = sb("weight", [P, TT, E])
        w_tok = sb("w_tok", [P, TT, P], F32R)
        wT = {k: sb(f"wT{k}", [P, BLK], F32R) for k in (1, 4)}

        raw_loaded = [sem(f"raw_loaded{n}") for n in range(NBATCH)]
        vec_loaded = sem("vec_loaded")
        pool_const = sem("pool_const")
        dve_const = sem("dve_const")
        a_done = sem("a_done")
        w_transposed = sem("w_transposed")
        w_hi_done = sem("w_hi_done")
        w_lo_done = sem("w_lo_done")
        wb_ready = sem("wb_ready")
        gate_ready = sem("gate_ready")
        up_ready = sem("up_ready")
        silu_done = sem("silu_done")
        weighted_done = sem("weighted_done")
        hid_done = sem("hid_done")
        hid_hi_done = sem("hid_hi_done")
        hid_lo_done = sem("hid_lo_done")
        down_done = sem("down_done")
        ffn_copied = {k: sem(f"ffn_copied{k}") for k in (1, 4)}
        ffn_transposed = {k: sem(f"ffn_transposed{k}") for k in (1, 4)}
        ffn_added = {k: sem(f"ffn_added{k}") for k in (1, 4)}
        ln_stats = {k: sem(f"ln_stats{k}") for k in LN}
        ln_scale = {k: sem(f"ln_scale{k}") for k in LN}
        xn_transposed = {k: sem(f"xn_transposed{k}") for k in (1, 2, 4)}
        xT_hi_done = {k: sem(f"xT_hi_done{k}") for k in (1, 2, 4)}
        xT_lo_done = {k: sem(f"xT_lo_done{k}") for k in (1, 2, 4)}
        logits_ready = {k: sem(f"logits_ready{k}") for k in (1, 4)}
        logit_silu_done = {k: sem(f"logit_silu_done{k}") for k in (1, 4)}
        route = {k: sem(f"route{k}") for k in (1, 4)}
        route_transposed = {k: sem(f"route_transposed{k}") for k in (1, 4)}
        wT_done = {k: sem(f"wT_done{k}") for k in (1, 4)}
        x_ln_loaded = sem("x_ln_loaded")
        x_res_loaded = sem("x_res_loaded")
        mix_gate_ready = sem("mix_gate_ready")
        mix_gate_done = sem("mix_gate_done")
        mix_val_ready = sem("mix_val_ready")
        mix_val_done = sem("mix_val_done")
        mix = sem("mix")
        y_hi_done = sem("y_hi_done")
        y_lo_done = sem("y_lo_done")
        mix_out_ready = sem("mix_out_ready")
        res_done = sem("res_done")
        x1_b_done = sem("x1_b_done")
        scaled_done = sem("scaled_done")
        x2_done = sem("x2_done")
        stored = sem("stored")

        ROUTE = 32
        LOGITS_READ = 2
        MIX = K + 2

        block = ctx.enter_context(nc.Block())

        setup_banks = [gate_ps[0], gate_ps[1], up_ps[0], up_ps[1]]

        def setup_bank(n):
            return setup_banks[n % len(setup_banks)][:, :]


        def is_block(b, n):
            return isinstance(b, int) and b == n

        def ffns_before(k, b):
            if k == 1:
                return 0 if is_block(b, 0) else b * 2 - 1
            return b * 2 + (1 if is_block(b, NBLK - 1) else 2)

        def first_tile(k, b):
            return ffns_before(k, b) * NT

        def first_pair(k, b):
            return ffns_before(k, b) * NPAIR

        def start_parity(k, b):
            if k == 1:
                return 0 if is_block(b, 0) else NT % 2
            return NT % 2 if is_block(b, NBLK - 1) else 0

        @block.sync
        def _(sp):
            def load_x_ln(b):
                if not is_block(b, 0):
                    sp.wait_ge(ln_scale[1], 4 * b)
                sp.dma_start(x_ln[:, :, :], x_blk[b]).then_inc(x_ln_loaded, 16)

            def load_x_res(b):
                if not is_block(b, 0):
                    sp.wait_ge(ffn_added[1], b)
                sp.dma_start(x_res[:, :, :], x_blk[b]).then_inc(x_res_loaded, 16)

            def store(b):
                sp.wait_ge(ffn_added[4], b + 1)
                sp.dma_start(out_blk[b], x3[:, :, :]).then_inc(stored, 16)

            load_x_ln(0)
            sp.dma_start(raw[:, WIN_G:WOUT, :], W_in.rearrange("(n p) h -> p n h", p=P))\
              .then_inc(raw_loaded[0], 16)
            sp.dma_start(raw[:, WOUT, :], W_out).then_inc(raw_loaded[0], 16)
            sp.wait_ge(dve_const, 1)
            sp.dma_start(raw[0:E, WROUTER, :], router_w).then_inc(raw_loaded[0], 16)
            gate_v = gate_w.rearrange("e i h -> (e i) h").rearrange("(n p) h -> p n h", p=P)
            up_v = up_w.rearrange("e i h -> (e i) h").rearrange("(n p) h -> p n h", p=P)
            down_v = down_w.rearrange("e h i -> h e i")
            for q in range(4):
                for n, (tile, view) in enumerate(((gate_tile, gate_v), (up_tile, up_v))):
                    sp.dma_start(raw[:, tile(4 * q):tile(4 * q) + 4, :], view[:, 4 * q:4 * q + 4, :])\
                      .then_inc(raw_loaded[1 + 3 * q + n], 16)
                dst = raw[:, down_tile(4 * q):down_tile(4 * q) + 4, :]
                sp.dma_start(dst.rearrange("p n (e i) -> p (n e) i", e=2), down_v[:, 8 * q:8 * q + 8, :])\
                  .then_inc(raw_loaded[3 + 3 * q], 16)
            for n, w in enumerate((sh_gate, sh_up, sh_down)):
                sp.dma_start(raw[:, 52 + n, :], w).then_inc(raw_loaded[NBATCH - 1], 16)
            load_x_res(0)
            load_x_ln(1)

            def step(i, first=False):
                load_x_res(i)
                load_x_ln(i + 1)
                store(i - 2)

            load_x_res(1)
            load_x_ln(2)
            with sp.Fori(2, NBLK - 1) as i:
                step(i)
            load_x_res(NBLK - 1)
            for b in range(NBLK - 3, NBLK):
                store(b)
            sp.wait_ge(stored, 16 * NBLK)

        @block.gpsimd
        def _(pool):
            pool.dma_start(bias_b[:, :], router_b.partition_broadcast(P)).then_inc(vec_loaded, 16)
            pool.dma_start(lnw_b[:, :], ln_w.partition_broadcast(P)).then_inc(vec_loaded, 16)
            pool.dma_start(lnb_b[:, :], ln_b.partition_broadcast(P)).then_inc(vec_loaded, 16)
            pool.dma_start(taps[:, :], conv_w.rearrange("d o k -> d (o k)")).then_inc(vec_loaded, 16)
            pool.dma_start(cbias[:, :], conv_b.unsqueeze(1)).then_inc(vec_loaded, 16)
            pool.dma_start(a_raw[:, :], a_param.unsqueeze(1)).then_inc(vec_loaded, 16)
            const = Steps(pool, pool_const, 0)
            const.done(nc.gpsimd.memset(zeros[:, :, :], 0.0))
            const.done(nc.gpsimd.memset(neg_half[:, :], -0.5))
            const.done(nc.gpsimd.memset(eps[:, :], EPS))
            const.wait()
            const.done(nc.gpsimd.affine_select(out=ident[:, :], in_=zeros[:, 0, :], fill=1.0,
                                               compare_op=ALU.not_equal, base=0,
                                               pattern=[[-1, P]], channel_multiplier=1))
            const.done(nc.gpsimd.affine_select(
                out=beat_at[:, :, :], in_=zeros[:, 0, 0:NG * NG].rearrange("p (g h) -> p g h", g=NG),
                fill=1e-37, compare_op=ALU.is_gt, base=0, pattern=[[1, NG], [-1, NG]], channel_multiplier=0))
            spread = [[-2, NPAIR], [-1, 2], [0, I]]
            as_rows = lambda t: t[:, :, :].rearrange("p n (e i) -> p n e i", e=2)
            const.done(nc.gpsimd.affine_select(out=as_rows(pick_half), in_=as_rows(zeros), fill=1.0,
                                               compare_op=ALU.not_equal, base=0,
                                               pattern=spread, channel_multiplier=1))
            const.wait()
            const.done(nc.gpsimd.affine_select(out=as_rows(pick), in_=as_rows(pick_half), fill=1.0,
                                               compare_op=ALU.not_equal, base=-E,
                                               pattern=spread, channel_multiplier=1))
            assert const.n == 7

            def hidden_low(k, b, j):
                n = first_tile(k, b) + j
                s = (start_parity(k, b) + j) % 2
                pool.wait_ge(hid_hi_done, n + 1)
                nc.gpsimd.tensor_tensor(hid_lo[s][:, :], hid[s][:, :], hid_hi[s][:, :].bitcast(F32),
                                        ALU.subtract).then_inc(hid_lo_done, 1)

            def norm_scale(k, b, src):
                st = Steps(pool, ln_scale[k], b * 4)
                pool.wait_ge(ln_stats[k], b * 2 + 2)
                st.done(nc.gpsimd.tensor_tensor(neg_mean[k][:, :], zeros[:, 0, 0:TT], meanvar[k][:, :, 0],
                                                ALU.subtract))
                st.done(nc.gpsimd.tensor_tensor(var_eps[k][:, :], meanvar[k][:, :, 1], eps[:, :], ALU.add))
                st.wait()
                st.done(nc.gpsimd.tensor_tensor(rstd[k][:, :], var_eps[k][:, :], neg_half[:, :], ALU.pow))
                st.wait()
                nc.gpsimd.tensor_tensor(pool_hold[:, :], zeros[:, 0, 0:1], zeros[:, 0, 0:1], ALU.add)
                for t in range(TT):
                    last = nc.gpsimd.tensor_scalar(normed[k][:, t, :], src[:, t, :], neg_mean[k][:, t:t + 1],
                                                   rstd[k][:, t:t + 1], ALU.add, ALU.mult)
                st.done(last)

            def ffn1_unit(i, main=True, tail=True):
                for j in range(NT):
                    if tail and j == 1:
                        pool.wait_ge(ln_scale[3], i * 4)
                        bc = lnw_b[:, :].unsqueeze(1).broadcast_to([P, TT, P])
                        nc.gpsimd.tensor_tensor(scaled[:, :, :], normed[3][:, :, :], bc, ALU.mult)\
                          .then_inc(scaled_done, 1)
                    if tail and j == 4:
                        norm_scale(4, i - 1, x2)
                    if main:
                        hidden_low(1, i, j)

            def ffn2_unit(i, main=True, chain=True, prepare=True):
                for j in range(NT):
                    if prepare and j == 0:
                        norm_scale(1, i + 1, x_ln)
                    if chain and j == 3:
                        norm_scale(2, i, x1)
                        bc = lnb_b[:, :].unsqueeze(1).broadcast_to([P, TT, P])
                        nc.gpsimd.tensor_tensor(x1_b[:, :, :], x1[:, :, :], bc, ALU.add).then_inc(x1_b_done, 1)
                    if chain and j == 12:
                        pool.wait_ge(y_hi_done, i + 1)
                        nc.gpsimd.tensor_tensor(y_lo[:, :], y[:, :], y_hi[:, :].bitcast(F32),
                                                ALU.subtract).then_inc(y_lo_done, 1)
                    if chain and j == 16:
                        norm_scale(3, i, res)
                    if main:
                        hidden_low(4, i - 1, j)

            norm_scale(1, 0, x_ln)
            pool.wait_ge(vec_loaded, 16 * 6)
            ffn1_unit(0, tail=False)
            ffn2_unit(0, main=False)
            ffn1_unit(1)
            ffn2_unit(1)
            with pool.Fori(2, NBLK - 1) as i:
                ffn1_unit(i)
                ffn2_unit(i)
            ffn1_unit(NBLK - 1)
            ffn2_unit(NBLK - 1, prepare=False)
            ffn1_unit(NBLK, main=False)
            ffn2_unit(NBLK, chain=False, prepare=False)

        @block.scalar
        def _(act):
            def weight_high(n):
                act.wait_ge(w_transposed, n + 1)
                nc.scalar.activation(wt_hi[:, 4 * n:4 * n + 4, :].rearrange("p n c -> p (n c)"),
                                     setup_bank(n), ACT.Copy).then_inc(w_hi_done, 1)

            def silu_tile(k, b, j):
                n = first_tile(k, b) + j
                s = (start_parity(k, b) + j) % 2
                act.wait_ge(gate_ready, n + 1)
                if not (isinstance(n, int) and n < 2):
                    act.wait_ge(hid_done, n - 1)
                nc.scalar.activation(silu_sb[s][:, :], gate_ps[s][:, :], ACT.Silu).then_inc(silu_done, 1)

            def hidden_high(k, b, j):
                n = first_tile(k, b) + j
                s = (start_parity(k, b) + j) % 2
                act.wait_ge(hid_done, n + 1)
                if not (isinstance(n, int) and n < 2):
                    act.wait_ge(down_done, n - 1)
                nc.scalar.activation(hid_hi[s][:, :], hid[s][:, :], ACT.Copy).then_inc(hid_hi_done, 1)

            def tile(k, b, j, before):
                silu_tile(k, b, j)
                if j > 0:
                    hidden_high(k, b, j - 1)
                elif before is not None:
                    hidden_high(*before, NT - 1)

            def ffn_copy(k, b):
                act.wait_ge(down_done, first_tile(k, b) + NT)
                nc.scalar.activation(ffn_sb[k][:, :], down_ps[:, :], ACT.Copy).then_inc(ffn_copied[k], 1)

            def xT_high(k, b):
                act.wait_ge(xn_transposed[k], b + 1)
                nc.scalar.activation(xT_hi[k][:, :], side[:, :], ACT.Copy).then_inc(xT_hi_done[k], 1)

            def silu_logits(k, b):
                act.wait_ge(route[k], b * ROUTE + 2)
                nc.scalar.activation(logit_silu[:, :, :], logit[:, :, :], ACT.Silu)\
                  .then_inc(logit_silu_done[k], 1)

            def wT_copy(k, b):
                act.wait_ge(route_transposed[k], b + 1)
                nc.scalar.activation(wT[k][:, :], side[:, :], ACT.Copy).then_inc(wT_done[k], 1)

            def ffn1_unit(i, main=True, tail=True, output=True):
                before = (4, i - 2) if output else None
                for j in range(NT):
                    if main:
                        tile(1, i, j, before)
                    if output and j == 2:
                        ffn_copy(4, i - 2)
                    if tail and j == 7:
                        xT_high(4, i - 1)
                    if tail and j == 9:
                        silu_logits(4, i - 1)
                    if tail and j == 16:
                        wT_copy(4, i - 1)

            def ffn2_unit(i, main=True, chain=True, prepare=True):
                for j in range(NT):
                    if main:
                        tile(4, i - 1, j, (1, i) if chain else None)
                    elif j == 0:
                        hidden_high(1, i, NT - 1)
                    if prepare and j == 1:
                        xT_high(1, i + 1)
                    if chain and j == 2:
                        ffn_copy(1, i)
                    if prepare and j == 6:
                        silu_logits(1, i + 1)
                    if chain and j == 7:
                        xT_high(2, i)
                    if chain and j == 9:
                        act.wait_ge(mix_gate_ready, i + 1)
                        nc.scalar.activation(gate_t[:, :], side[:, :], ACT.Tanh, scale=0.5)\
                          .then_inc(mix_gate_done, 1)
                    if chain and j == 10:
                        act.wait_ge(mix_val_ready, i + 1)
                        nc.scalar.activation(val_pad[:, :, PADK:PADK + SEQ],
                                             side[:, :].rearrange("p (s t) -> p s t", s=SB), ACT.Copy)\
                          .then_inc(mix_val_done, 1)
                    if chain and j == 12:
                        act.wait_ge(mix, i * MIX + MIX)
                        nc.scalar.activation(y_hi[:, :], y[:, :], ACT.Copy).then_inc(y_hi_done, 1)
                    if prepare and j == 14:
                        wT_copy(1, i + 1)

            act.wait_ge(vec_loaded, 16 * 6)
            nc.scalar.activation(a_tanh[:, :], a_raw[:, :], ACT.Tanh).then_inc(a_done, 1)
            for n in range(NBATCH):
                weight_high(n)
                if n == 0:
                    xT_high(1, 0)
                if n == 1:
                    silu_logits(1, 0)
            wT_copy(1, 0)
            ffn1_unit(0, tail=False, output=False)
            ffn2_unit(0, main=False)
            ffn1_unit(1, output=False)
            ffn2_unit(1)
            with act.Fori(2, NBLK - 1) as i:
                ffn1_unit(i)
                ffn2_unit(i)
            ffn1_unit(NBLK - 1)
            ffn2_unit(NBLK - 1, prepare=False)
            hidden_high(4, NBLK - 2, NT - 1)
            ffn1_unit(NBLK, main=False)
            ffn2_unit(NBLK, chain=False, prepare=False)
            hidden_high(4, NBLK - 1, NT - 1)
            ffn_copy(4, NBLK - 1)

        @block.vector
        def _(dve):
            V = nc.vector

            def weight_low(n):
                dve.wait_ge(w_hi_done, n + 1)
                V.tensor_tensor(wt_lo[:, 4 * n:4 * n + 4, :].rearrange("p n c -> p (n c)"), setup_bank(n),
                                wt_hi[:, 4 * n:4 * n + 4, :].rearrange("p n c -> p (n c)").bitcast(F32),
                                ALU.subtract).then_inc(w_lo_done, 1)

            def weigh_tile(k, b, j):
                n = first_tile(k, b) + j
                s = (start_parity(k, b) + j) % 2
                dve.wait_ge(silu_done, n + 1)
                dve.wait_ge(wb_ready, first_pair(k, b) + j + 1)
                V.tensor_tensor(weighted[s][:, :], silu_sb[s][:, :], wb_ps[j % 2][:, :], ALU.mult)\
                 .then_inc(weighted_done, 1)

            def hidden_tile(k, b, j):
                n = first_tile(k, b) + j
                s = (start_parity(k, b) + j) % 2
                dve.wait_ge(up_ready, n + 1)
                if j < NPAIR:
                    dve.wait_ge(weighted_done, first_pair(k, b) + j + 1)
                else:
                    dve.wait_ge(silu_done, n + 1)
                if not (isinstance(n, int) and n < 2):
                    dve.wait_ge(hid_lo_done, n - 1)
                factor = weighted[s] if j < NPAIR else silu_sb[s]
                V.tensor_tensor(hid[s][:, :], factor[:, :], up_ps[s][:, :], ALU.mult).then_inc(hid_done, 1)

            def norm_stats(k, b, src):
                for t in range(TT):
                    last = V.bn_stats(stats[k][:, t, :], src[:, t, :])
                last.then_inc(ln_stats[k], 1)
                dve.wait_ge(ln_stats[k], b * 2 + 1)
                V.memset(hold[:, :], 0.0)
                for t in range(TT):
                    last = V.bn_aggr(meanvar[k][:, t, :], stats[k][:, t, :])
                last.then_inc(ln_stats[k], 1)

            def xT_low(k, b):
                dve.wait_ge(xT_hi_done[k], b + 1)
                V.tensor_tensor(xT_lo[k][:, :], side[:, :], xT_hi[k][:, :].bitcast(F32), ALU.subtract)\
                 .then_inc(xT_lo_done[k], 1)

            def route_logits(k, b, st):
                dve.wait_ge(logits_ready[k], b + 1)
                st.done(V.tensor_scalar(tiny[:, :, :], side_te, -1e-9, 1e-8, ALU.is_ge, ALU.mult))
                st.wait()
                st.done(V.tensor_tensor(logit[:, :, :], tiny[:, :, :], side_te, ALU.add))
                st.wait()
                st.done(V.reciprocal(logit_inv[:, :, :], logit[:, :, :]))

            def route_scores(k, b, st):
                dve.wait_ge(logit_silu_done[k], b + 1)
                st.wait()
                st.done(V.tensor_tensor(score[:, :, :], logit_silu[:, :, :], logit_inv[:, :, :], ALU.mult))
                st.wait()
                st.done(V.tensor_tensor(biased[:, :, :], score[:, :, :],
                                        bias_b[:, :].unsqueeze(1).broadcast_to([P, TT, E]), ALU.add))
                st.wait()
                g8 = biased[:, :, :].rearrange("p t (g c) -> p (t g) c", g=NG)
                st.done(V.tensor_tensor(hi4[:, :, :], g8[:, :, 0:4], g8[:, :, 4:8], ALU.max))
                st.done(V.tensor_tensor(lo4[:, :, :], g8[:, :, 0:4], g8[:, :, 4:8], ALU.min))

            def route_merge(st):
                st.wait()
                st.done(V.tensor_tensor(hi2[:, :, :], hi4[:, :, 0:2], hi4[:, :, 2:4], ALU.max))
                st.done(V.tensor_tensor(lo2a[:, :, :], hi4[:, :, 0:2], hi4[:, :, 2:4], ALU.min))
                st.done(V.tensor_tensor(lo2b[:, :, :], lo4[:, :, 0:2], lo4[:, :, 2:4], ALU.max))
                st.wait()
                st.done(V.tensor_tensor(lo2[:, :, :], lo2a[:, :, :], lo2b[:, :, :], ALU.max))
                st.wait()
                st.done(V.tensor_tensor(hi1[:, :, :], hi2[:, :, 0:1], hi2[:, :, 1:2], ALU.max))
                st.done(V.tensor_tensor(lo1a[:, :, :], hi2[:, :, 0:1], hi2[:, :, 1:2], ALU.min))
                st.done(V.tensor_tensor(lo1b[:, :, :], lo2[:, :, 0:1], lo2[:, :, 1:2], ALU.max))
                st.wait()
                st.done(V.tensor_tensor(lo1[:, :, :], lo1a[:, :, :], lo1b[:, :, :], ALU.max))
                st.wait()
                st.done(V.tensor_tensor(gsum[:, :, :].rearrange("p t g -> p (t g)").unsqueeze(2),
                                        hi1[:, :, :], lo1[:, :, :], ALU.add))

            def route_groups(st):
                st.wait()
                for t in range(TT):
                    last = V.tensor_tensor(gdiff[:, t, :].rearrange("p (g h) -> p g h", g=NG),
                                           gsum[:, t, :].unsqueeze(1).broadcast_to([P, NG, NG]),
                                           gsum[:, t, :].unsqueeze(2).broadcast_to([P, NG, NG]), ALU.subtract)
                st.done(last)
                st.wait()
                st.done(V.tensor_tensor(beats[:, :, :].rearrange("p (t g) h -> p t (g h)", t=TT), gdiff[:, :, :],
                                        beat_at[:, :, :].rearrange("p g h -> p (g h)").unsqueeze(1)
                                        .broadcast_to([P, TT, NG * NG]), ALU.is_ge))
                st.wait()
                st.done(V.tensor_reduce(grank[:, :], beats[:, :, :], AX.X, ALU.add))
                st.wait()
                st.done(V.tensor_scalar(gmask[:, :], grank[:, :], float(GTOP), None, ALU.is_lt))
                st.wait()
                st.done(V.tensor_tensor(masked0[:, :, :].rearrange("p t (g c) -> p (t g) c", g=NG),
                                        biased[:, :, :].rearrange("p t (g c) -> p (t g) c", g=NG),
                                        gmask[:, :].unsqueeze(2).broadcast_to([P, TT * NG, PG]), ALU.mult))
                st.wait()
                st.done(V.tensor_scalar(masked[:, :, 0:E], masked0[:, :, :], 0.0, None, ALU.add))

            def route_top(st):
                st.wait()
                V.memset(hold[:, :], 0.0)
                for t in range(TT):
                    last = V.max(top8[:, t, :], masked[:, t, 0:E])
                st.done(last)
                st.wait()
                st.done(V.memset(top8[:, :, TOP:8], FAR))
                st.wait()
                V.memset(hold[:, :], 0.0)
                for t in range(TT):
                    last = V.match_replace(replaced[:, t, :], top8[:, t, :], masked[:, t, :], GONE)
                st.done(last)
                st.wait()
                st.done(V.scalar_tensor_tensor(chosen[:, :, :], replaced[:, :, 0:E], (FAR + GONE) / 2,
                                               score[:, :, :], ALU.is_lt, ALU.mult))
                st.wait()
                st.done(V.tensor_reduce(wsum[:, :], chosen[:, :, :], AX.X, ALU.add))

            def route_weights(k, b, st):
                st.wait()
                st.done(V.tensor_scalar(wsum_e[:, :], wsum[:, :], 1e-20, None, ALU.add))
                st.wait()
                st.done(V.reciprocal(winv[:, :], wsum_e[:, :]))
                st.wait()
                st.done(V.scalar_tensor_tensor(weight[:, :, :], chosen[:, :, :], SCALE,
                                               winv[:, :].unsqueeze(2).broadcast_to([P, TT, E]), ALU.mult, ALU.mult))
                st.wait()
                st.done(V.tensor_copy(w_tok[:, :, 0:E], weight[:, :, :]))
                st.wait()
                st.done(V.tensor_tensor(w_tok[:, :, E:2 * E], weight[:, :, :], w_tok[:, :, 0:E].bitcast(F32),
                                        ALU.subtract))

            def route_end(st):
                assert st.n == ROUTE

            def conv_tap(i, st, t):
                src = val_pad[:, :, t:t + SEQ]
                if t == 0:
                    dve.wait_ge(mix_val_done, i + 1)
                    st.done(V.tensor_scalar(conv[0][:, :, :], src, taps_half[:, 0:1], cbias_half[:, 0:1],
                                            ALU.mult, ALU.add))
                else:
                    st.wait()
                    st.done(V.scalar_tensor_tensor(conv[t % 2][:, :, :], src, taps_half[:, t:t + 1],
                                                   conv[(t + 1) % 2][:, :, :], ALU.mult, ALU.add))

            def recur(i, st):
                dve.wait_ge(mix_gate_done, i + 1)
                st.wait()
                st.done(V.scalar_tensor_tensor(gated[:, :].rearrange("p (s t) -> p s t", s=SB),
                                               gate_t[:, :].rearrange("p (s t) -> p s t", s=SB), 1.0,
                                               conv[(K - 1) % 2][:, :, :], ALU.add, ALU.mult))
                st.wait()
                if not is_block(i, 0):
                    dve.wait_ge(y_lo_done, i)
                st.done(V.tensor_tensor_scan(y[:, :], decay[:, :], gated[:, :], 0.0, ALU.mult, ALU.add))
                assert st.n == MIX

            def ffn_add(k, b, residual, dst):
                dve.wait_ge(ffn_transposed[k], b + 1)
                V.scalar_tensor_tensor(dst[:, :, :], side_td, 0.5, residual[:, :, :], ALU.mult, ALU.add)\
                 .then_inc(ffn_added[k], 1)

            def ffn1_unit(i, main=True, tail=True, output=True):
                st = Steps(dve, route[4], (i - 1) * ROUTE) if tail else None
                for j in range(NT):
                    if main and j < NPAIR:
                        weigh_tile(1, i, j)
                    if tail and j == 9:
                        route_scores(4, i - 1, st)
                    if tail and j == 10:
                        route_merge(st)
                    if tail and j == 12:
                        route_groups(st)
                    if tail and j == 14:
                        route_weights(4, i - 1, st)
                        route_end(st)
                    if main:
                        hidden_tile(1, i, j)
                    if output and j == 3:
                        if not is_block(i, 2):
                            dve.wait_ge(stored, (i - 2) * 16)
                        ffn_add(4, i - 2, x2, x3)
                    if tail and j == 3:
                        dve.wait_ge(scaled_done, i)
                        dve.wait_ge(x1_b_done, i)
                        if not is_block(i, 1):
                            dve.wait_ge(ffn_added[4], i - 1)
                        V.tensor_tensor(x2[:, :, :], scaled[:, :, :], x1_b[:, :, :], ALU.add).then_inc(x2_done, 1)
                        dve.wait_ge(x2_done, i)
                        norm_stats(4, i - 1, x2)
                    if tail and j == 7:
                        xT_low(4, i - 1)
                    if tail and j == 8:
                        route_logits(4, i - 1, st)
                    if tail and j == 13:
                        route_top(st)

            def ffn2_unit(i, main=True, chain=True, prepare=True):
                st = Steps(dve, route[1], (i + 1) * ROUTE) if prepare else None
                mx = Steps(dve, mix, i * MIX) if chain else None
                for j in range(NT):
                    if main and j < NPAIR:
                        weigh_tile(4, i - 1, j)
                    if prepare and j == 6:
                        route_scores(1, i + 1, st)
                    if prepare and j == 7:
                        route_merge(st)
                    if prepare and j == 8:
                        route_groups(st)
                    if chain and j == 10:
                        conv_tap(i, mx, 0)
                        conv_tap(i, mx, 1)
                    if chain and j == 11:
                        conv_tap(i, mx, 4)
                        recur(i, mx)
                    if prepare and j == 13:
                        route_weights(1, i + 1, st)
                        route_end(st)
                    if main:
                        hidden_tile(4, i - 1, j)
                    if prepare and j == 1:
                        xT_low(1, i + 1)
                    if chain and j == 3:
                        dve.wait_ge(x_res_loaded, i * 16 + 16)
                        ffn_add(1, i, x_res, x1)
                        dve.wait_ge(ffn_added[1], i + 1)
                        norm_stats(2, i, x1)
                    if prepare and j == 5:
                        route_logits(1, i + 1, st)
                    if chain and j == 7:
                        xT_low(2, i)
                    if chain and j == 10:
                        conv_tap(i, mx, 2)
                        conv_tap(i, mx, 3)
                    if prepare and j == 12:
                        route_top(st)
                    if chain and j == 15:
                        dve.wait_ge(mix_out_ready, i + 1)
                        V.tensor_tensor(res[:, :, :], side_td, normed[2][:, :, :], ALU.add).then_inc(res_done, 1)
                        dve.wait_ge(res_done, i + 1)
                        norm_stats(3, i, res)
                    if chain and j == 16 and not (isinstance(i, int) and i > NBLK - 3):
                        dve.wait_ge(x_ln_loaded, i * 16 + 48)
                        norm_stats(1, i + 2, x_ln)

            const = Steps(dve, dve_const, 0)
            const.done(V.memset(raw[:, WROUTER, :], 0.0))
            const.done(V.memset(val_pad[:, :, :], 0.0))
            const.done(V.memset(masked[:, :, :], FAR))
            const.done(V.memset(ones[:, :], 1.0))
            const.done(V.memset(w_tok[:, :, :].bitcast(F32), 0.0))
            dve.wait_ge(x_ln_loaded, 16)
            norm_stats(1, 0, x_ln)
            dve.wait_ge(vec_loaded, 16 * 6)
            const.done(V.tensor_scalar(taps_half[:, :], taps[:, :], 0.5, None, ALU.mult))
            const.done(V.tensor_scalar(cbias_half[:, :], cbias[:, :], 0.5, None, ALU.mult))
            dve.wait_ge(a_done, 1)
            const.wait()
            const.done(V.tensor_scalar(decay[:, :], ones[:, :], a_tanh[:, 0:1], None, ALU.mult))
            const.wait()
            const.done(V.memset(decay[:, :].rearrange("p (s t) -> p s t", s=SB)[:, :, 0:1], 0.0))
            const.wait()
            first = Steps(dve, route[1], 0)
            for n in range(NBATCH):
                weight_low(n)
                if n == 0:
                    xT_low(1, 0)
                if n == 1:
                    route_logits(1, 0, first)
                if n == 2:
                    route_scores(1, 0, first)
                    route_merge(first)
                    route_groups(first)
                    route_top(first)
                    route_weights(1, 0, first)
                    route_end(first)
            dve.wait_ge(x_ln_loaded, 32)
            norm_stats(1, 1, x_ln)
            ffn1_unit(0, tail=False, output=False)
            ffn2_unit(0, main=False)
            ffn1_unit(1, output=False)
            ffn2_unit(1)
            with dve.Fori(2, NBLK - 2) as i:
                ffn1_unit(i)
                ffn2_unit(i)
            ffn1_unit(NBLK - 2)
            ffn2_unit(NBLK - 2)
            ffn1_unit(NBLK - 1)
            ffn2_unit(NBLK - 1, prepare=False)
            ffn1_unit(NBLK, main=False)
            ffn2_unit(NBLK, chain=False, prepare=False)
            dve.wait_ge(stored, 16 * (NBLK - 1))
            ffn_add(4, NBLK - 1, x2, x3)

        @block.tensor
        def _(pe):
            def product(dst, w, moving_hi, moving_lo, w_lo, start, stop):
                nc.tensor.matmul(dst, w, moving_hi, start=start, stop=False)
                nc.tensor.matmul(dst, w, moving_lo, start=False, stop=False)
                return nc.tensor.matmul(dst, w_lo, moving_hi, start=False, stop=stop)

            def weights(n):
                pe.wait_ge(raw_loaded[n], {0: 48, NBATCH - 1: 48}.get(n, 16))
                if n >= len(setup_banks):
                    pe.wait_ge(w_lo_done, n - len(setup_banks) + 1)
                for t in range(4):
                    if 4 * n + t <= down_tile(NPAIR):
                        last = nc.tensor.transpose(setup_bank(n)[:, t * P:(t + 1) * P], raw[:, 4 * n + t, :],
                                                   ident[:, :])
                    else:
                        last = nc.tensor.transpose(setup_bank(n)[:, t * P:(t + 1) * P], raw[:, WROUTER, :],
                                                   ident[:, :])
                last.then_inc(w_transposed, 1)

            def spread_weights(k, b, j):
                r = first_pair(k, b) + j
                if not (isinstance(r, int) and r < 2):
                    pe.wait_ge(weighted_done, r - 1)
                nc.tensor.matmul(wb_ps[j % 2][:, :], pick[:, j, :], wT[k][:, :], start=True, stop=True)\
                  .then_inc(wb_ready, 1)

            def up_tiles(k, b, j):
                n = first_tile(k, b) + j
                s = (start_parity(k, b) + j) % 2
                late = not (isinstance(n, int) and n < 2)
                if j < NPAIR:
                    spread_weights(k, b, j)
                if late:
                    pe.wait_ge(silu_done, n - 1)
                g, u = gate_tile(j), up_tile(j)
                product(gate_ps[s][:, :], wt_hi[:, g, :], xT_hi[k][:, :], xT_lo[k][:, :], wt_lo[:, g, :],
                        True, True).then_inc(gate_ready, 1)
                if late:
                    pe.wait_ge(hid_done, n - 1)
                product(up_ps[s][:, :], wt_hi[:, u, :], xT_hi[k][:, :], xT_lo[k][:, :], wt_lo[:, u, :],
                        True, True).then_inc(up_ready, 1)

            def down(k, b, j):
                n = first_tile(k, b) + j
                s = (start_parity(k, b) + j) % 2
                w = down_tile(j)
                if j == 0:
                    if k == 4:
                        pe.wait_ge(ffn_copied[1], b + 2 if not is_block(b, NBLK - 1) else b + 1)
                    elif not is_block(b, 0):
                        if is_block(b, 1):
                            pe.wait_ge(ffn_copied[1], 1)
                        else:
                            pe.wait_ge(ffn_copied[4], b - 1)
                pe.wait_ge(hid_hi_done, n + 1)
                nc.tensor.matmul(down_ps[:, :], wt_hi[:, w, :], hid_hi[s][:, :], start=(j == 0), stop=False)
                nc.tensor.matmul(down_ps[:, :], wt_lo[:, w, :], hid_hi[s][:, :], start=False, stop=False)
                pe.wait_ge(hid_lo_done, n + 1)
                nc.tensor.matmul(down_ps[:, :], wt_hi[:, w, :], hid_lo[s][:, :], start=False,
                                 stop=(j == NT - 1)).then_inc(down_done, 1)

            def transpose4(src, done):
                for t in range(TT):
                    last = nc.tensor.transpose(side[:, t * P:(t + 1) * P], src(t), ident[:, :])
                last.then_inc(done, 1)

            def transpose_norm(k, b):
                pe.wait_ge(ln_scale[k], b * 4 + 4)
                transpose4(lambda t: normed[k][:, t, :], xn_transposed[k])

            def transpose_ffn(k, b):
                pe.wait_ge(ffn_copied[k], b + 1)
                transpose4(lambda t: ffn_sb[k][:, t * P:(t + 1) * P], ffn_transposed[k])

            def router(k, b):
                for t in range(TT):
                    dst = side[:, t * E:(t + 1) * E]
                    hi, lo = xT_hi[k][:, t * P:(t + 1) * P], xT_lo[k][:, t * P:(t + 1) * P]
                    w_h, w_l = wt_hi[:, WROUTER, 0:E], wt_lo[:, WROUTER, 0:E]
                    nc.tensor.matmul(dst, hi, w_h, start=True, stop=False)
                    nc.tensor.matmul(dst, hi, w_l, start=False, stop=False)
                    nc.tensor.matmul(dst, lo, w_h, start=False, stop=False)
                    last = nc.tensor.matmul(dst, lo, w_l, start=False, stop=True)
                last.then_inc(logits_ready[k], 1)

            def transpose_route(k, b):
                pe.wait_ge(route[k], b * ROUTE + ROUTE)
                transpose4(lambda t: w_tok[:, t, :].bitcast(F32), route_transposed[k])

            def ffn1_unit(i, main=True, tail=True, output=True):
                if main:
                    pe.wait_ge(xT_lo_done[1], i + 1)
                    pe.wait_ge(wT_done[1], i + 1)
                for j in range(NT):
                    if main:
                        up_tiles(1, i, j)
                        if j >= 2:
                            down(1, i, j - 2)
                        elif output:
                            down(4, i - 2, NT - 2 + j)
                    if output and j == 3:
                        pe.wait_ge(res_done, i)
                        transpose_ffn(4, i - 2)
                    if tail and j == 6:
                        if output:
                            pe.wait_ge(ffn_added[4], i - 1)
                        else:
                            pe.wait_ge(res_done, i)
                        transpose_norm(4, i - 1)
                    if tail and j == 8:
                        pe.wait_ge(xT_lo_done[4], i)
                        router(4, i - 1)
                    if tail and j == 15:
                        transpose_route(4, i - 1)

            def ffn2_unit(i, main=True, chain=True, prepare=True):
                if main:
                    pe.wait_ge(xT_lo_done[4], i)
                    pe.wait_ge(wT_done[4], i)
                for j in range(NT):
                    if main:
                        up_tiles(4, i - 1, j)
                        if j >= 2:
                            down(4, i - 1, j - 2)
                        elif chain:
                            down(1, i, NT - 2 + j)
                    elif j < 2:
                        down(1, i, NT - 2 + j)
                    if prepare and j == 0:
                        if main:
                            pe.wait_ge(wT_done[4], i)
                        else:
                            pe.wait_ge(wT_done[1], 1)
                        transpose_norm(1, i + 1)
                    if chain and j == 3:
                        if prepare:
                            pe.wait_ge(xT_lo_done[1], i + 2)
                        else:
                            pe.wait_ge(wT_done[4], i)
                        transpose_ffn(1, i)
                    if prepare and j == 5:
                        pe.wait_ge(ffn_added[1], i + 1)
                        router(1, i + 1)
                    if chain and j == 6:
                        if prepare:
                            pe.wait_ge(route[1], (i + 1) * ROUTE + LOGITS_READ)
                        else:
                            pe.wait_ge(ffn_added[1], i + 1)
                        transpose_norm(2, i)
                    if chain and j == 8:
                        pe.wait_ge(xT_lo_done[2], i + 1)
                        product(side[:, :], wt_hi[:, WIN_G, :], xT_hi[2][:, :], xT_lo[2][:, :], wt_lo[:, WIN_G, :],
                                True, True).then_inc(mix_gate_ready, 1)
                    if chain and j == 9:
                        pe.wait_ge(mix_gate_done, i + 1)
                        product(side[:, :], wt_hi[:, WIN_V, :], xT_hi[2][:, :], xT_lo[2][:, :], wt_lo[:, WIN_V, :],
                                True, True).then_inc(mix_val_ready, 1)
                    if prepare and j == 13:
                        pe.wait_ge(mix_val_done, i + 1)
                        transpose_route(1, i + 1)
                    if chain and j == 15:
                        if prepare:
                            pe.wait_ge(wT_done[1], i + 2)
                        else:
                            pe.wait_ge(mix_val_done, i + 1)
                        pe.wait_ge(y_lo_done, i + 1)
                        for t in range(TT):
                            rows = slice(t * P, (t + 1) * P)
                            nc.tensor.matmul(side[:, rows], y_hi[:, rows], wt_hi[:, WOUT, :], start=True, stop=False)
                            nc.tensor.matmul(side[:, rows], y_hi[:, rows], wt_lo[:, WOUT, :], start=False, stop=False)
                            last = nc.tensor.matmul(side[:, rows], y_lo[:, rows], wt_hi[:, WOUT, :],
                                                    start=False, stop=True)
                        last.then_inc(mix_out_ready, 1)

            pe.wait_ge(pool_const, 7)
            pe.wait_ge(dve_const, 5)
            weights(0)
            transpose_norm(1, 0)
            weights(1)
            pe.wait_ge(xT_lo_done[1], 1)
            pe.wait_ge(w_lo_done, 1)
            router(1, 0)
            for n in range(2, NBATCH):
                weights(n)
            transpose_route(1, 0)
            pe.wait_ge(w_lo_done, NBATCH)
            ffn1_unit(0, tail=False, output=False)
            ffn2_unit(0, main=False)
            ffn1_unit(1, output=False)
            ffn2_unit(1)
            with pe.Fori(2, NBLK - 1) as i:
                ffn1_unit(i)
                ffn2_unit(i)
            ffn1_unit(NBLK - 1)
            ffn2_unit(NBLK - 1, prepare=False)
            down(4, NBLK - 2, NT - 2)
            down(4, NBLK - 2, NT - 1)
            ffn1_unit(NBLK, main=False)
            ffn2_unit(NBLK, chain=False, prepare=False)
            down(4, NBLK - 1, NT - 2)
            down(4, NBLK - 1, NT - 1)
            pe.wait_ge(ffn_added[4], NBLK - 1)
            transpose_ffn(4, NBLK - 1)


_INS = ["L0_attn_x", "L0_attn_W_in", "L0_attn_conv_w", "L0_attn_conv_b", "L0_attn_a_param", "L0_attn_W_out",
        "L0_attn_ln_w", "L0_attn_ln_b", "L0_ffn_router_weight", "L0_ffn_router_bias", "L0_ffn_gate_w",
        "L0_ffn_up_w", "L0_ffn_down_w", "L0_ffn_shared_gate_w", "L0_ffn_shared_up_w", "L0_ffn_shared_down_w"]


def kernel(**inputs):
    import numpy as np
    import concourse.bacc as bacc
    from concourse.bass_utils import run_bass_kernel_spmd

    nc = bacc.Bacc("TRN2", target_bir_lowering=False, num_devices=1)
    arrays, args = {}, []
    for name in _INS:
        a = np.ascontiguousarray(inputs[name])
        arrays[f"in_{name}"] = a
        args.append(nc.dram_tensor(f"in_{name}", a.shape, mybir.dt.from_np(a.dtype), kind="ExternalInput").ap())
    shape = arrays["in_L0_attn_x"].shape
    out = nc.dram_tensor("out_x", shape, F32, kind="ExternalOutput").ap()
    macaron_kernel(nc, *args, out)
    r = run_bass_kernel_spmd(nc, [arrays], core_ids=[0])
    return r.results[0]["out_x"]
```

```python
from contextlib import ExitStack

import concourse.bass as bass
from concourse import mybir

F32 = mybir.dt.float32
F32R = mybir.dt.float32r
ALU = mybir.AluOpType
ACT = mybir.ActivationFunctionType
AX = mybir.AxisListType

P = 128
SEQS, SEQ = 16, 256
BLK = 512
NBLK = SEQS * SEQ // BLK
TT = BLK // P
SB = BLK // SEQ
E, I = 32, 64
NPAIR = E * I // P
NT = NPAIR + 1
NG, PG = 4, E // 4
GTOP, TOP = 2, 4
SCALE = 2.5
K = 5
PADK = K // 2
EPS = 1e-5
FAR, GONE = -2.0e38, -3.0e38
LAG = 3
RING = 3
NBATCH = 14


def gate_tile(j):
    return 4 + 12 * (j // 4) + j % 4 if j < NPAIR else 52


def up_tile(j):
    return gate_tile(j) + (4 if j < NPAIR else 1)


def down_tile(j):
    return gate_tile(j) + (8 if j < NPAIR else 2)


WIN_G, WIN_V, WOUT, WROUTER = 0, 1, 2, 3


class Steps:

    def __init__(self, engine, sem, base):
        self.engine, self.sem, self.base, self.n = engine, sem, base, 0

    def done(self, instruction):
        instruction.then_inc(self.sem, 1)
        self.n += 1

    def wait(self):
        self.engine.wait_ge(self.sem, self.base + self.n)


def macaron_kernel(nc, x, W_in, conv_w, conv_b, a_param, W_out, ln_w, ln_b, router_w, router_b,
                   gate_w, up_w, down_w, sh_gate, sh_up, sh_down, out):
    x_blk = x.rearrange("a s d -> (a s) d").rearrange("(n t p) d -> n p t d", t=TT, p=P)
    out_blk = out.rearrange("a s d -> (a s) d").rearrange("(n t p) d -> n p t d", t=TT, p=P)

    with ExitStack() as ctx:
        def sb(name, shape, dt=F32):
            return ctx.enter_context(nc.sbuf_tensor(name, shape, dt))

        def psum(name):
            return ctx.enter_context(nc.psum_tensor(name, [P, BLK], F32))

        def sem(name):
            return ctx.enter_context(nc.semaphore(name))

        gate_ps = [psum("gate_ps0"), psum("gate_ps1")]
        up_ps = [psum("up_ps0"), psum("up_ps1")]
        wb_ps = [psum("wb_ps0"), psum("wb_ps1")]
        down_ps = psum("down_ps")
        side = psum("side")
        side_td = side[:, :].rearrange("p (t d) -> p t d", t=TT)
        side_te = side_td[:, :, 0:E]

        raw = sb("raw", [P, NBATCH * 4, P])
        wt_hi = sb("wt_hi", [P, NBATCH * 4, P], F32R)
        wt_lo = sb("wt_lo", [P, NBATCH * 4, P], F32R)
        ident = sb("ident", [P, P])
        zeros = sb("zeros", [P, P])
        pick_half = sb("pick_half", [P, NPAIR, P])
        pick = sb("pick", [P, NPAIR, P], F32R)
        neg_half = sb("neg_half", [P, TT])
        eps = sb("eps", [P, TT])
        hold = sb("hold", [P, 1])
        beat_at = sb("beat_at", [P, NG, NG])
        bias_b = sb("bias_b", [P, E])
        lnw_b = sb("lnw_b", [P, P])
        lnb_b = sb("lnb_b", [P, P])
        taps = sb("taps", [P, K])
        taps_half = sb("taps_half", [P, K])
        cbias = sb("cbias", [P, 1])
        cbias_half = sb("cbias_half", [P, 1])
        a_raw = sb("a_raw", [P, 1])
        a_tanh = sb("a_tanh", [P, 1])
        ones = sb("ones", [P, BLK])
        decay = sb("decay", [P, BLK])
        silu_sb = [sb("silu_sb0", [P, BLK]), sb("silu_sb1", [P, BLK])]
        weighted = [sb("weighted0", [P, BLK]), sb("weighted1", [P, BLK])]
        hid = [sb(f"hid{n}", [P, BLK]) for n in range(RING)]
        hid_hi = [sb(f"hid_hi{n}", [P, BLK], F32R) for n in range(RING)]
        hid_lo = [sb(f"hid_lo{n}", [P, BLK], F32R) for n in range(RING)]
        LN = (1, 2, 3, 4)
        stats = {k: sb(f"stats{k}", [P, TT, 6]) for k in LN}
        meanvar = {k: sb(f"meanvar{k}", [P, TT, 2]) for k in LN}
        var_eps = {k: sb(f"var_eps{k}", [P, TT]) for k in LN}
        neg_mean = {k: sb(f"neg_mean{k}", [P, TT]) for k in LN}
        shift = {k: sb(f"shift{k}", [P, TT]) for k in LN}
        rstd = {k: sb(f"rstd{k}", [P, TT]) for k in LN}
        normed = {k: sb(f"normed{k}", [P, TT, P]) for k in LN}
        xT_hi = {k: sb(f"xT_hi{k}", [P, BLK], F32R) for k in (1, 2, 4)}
        xT_lo = {k: sb(f"xT_lo{k}", [P, BLK], F32R) for k in (1, 2, 4)}
        x_ln = sb("x_ln", [P, TT, P])
        x_res = sb("x_res", [P, TT, P])
        x1 = sb("x1", [P, TT, P])
        x1_b = sb("x1_b", [P, TT, P])
        x2 = sb("x2", [P, TT, P])
        x2_kept = sb("x2_kept", [P, TT, P])
        x3 = sb("x3", [P, TT, P])
        ffn_sb = {k: sb(f"ffn_sb{k}", [P, BLK]) for k in (1, 4)}
        gate_t = sb("gate_t", [P, BLK])
        val_pad = sb("val_pad", [P, SB, SEQ + 2 * PADK])
        conv = [sb("conv0", [P, SB, SEQ]), sb("conv1", [P, SB, SEQ])]
        gated = sb("gated", [P, BLK])
        y = sb("y", [P, BLK])
        y_hi = sb("y_hi", [P, BLK], F32R)
        y_lo = sb("y_lo", [P, BLK], F32R)
        res = sb("res", [P, TT, P])
        scaled = sb("scaled", [P, TT, P])
        logitsT = sb("logitsT", [P, BLK])
        tiny = sb("tiny", [P, TT, E])
        logit = sb("logit", [P, TT, E])
        logit_silu = sb("logit_silu", [P, TT, E])
        logit_inv = sb("logit_inv", [P, TT, E])
        score = sb("score", [P, TT, E])
        biased = sb("biased", [P, TT, E])
        hi4 = sb("hi4", [P, TT * NG, 4])
        lo4 = sb("lo4", [P, TT * NG, 4])
        hi2 = sb("hi2", [P, TT * NG, 2])
        lo2a = sb("lo2a", [P, TT * NG, 2])
        lo2b = sb("lo2b", [P, TT * NG, 2])
        lo2 = sb("lo2", [P, TT * NG, 2])
        hi1 = sb("hi1", [P, TT * NG, 1])
        lo1a = sb("lo1a", [P, TT * NG, 1])
        lo1b = sb("lo1b", [P, TT * NG, 1])
        lo1 = sb("lo1", [P, TT * NG, 1])
        gsum = sb("gsum", [P, TT, NG])
        gdiff = sb("gdiff", [P, TT, NG * NG])
        beats = sb("beats", [P, TT * NG, NG])
        grank = sb("grank", [P, TT * NG])
        gmask = sb("gmask", [P, TT * NG])
        masked0 = sb("masked0", [P, TT, E])
        masked = sb("masked", [P, TT, E + TOP])
        top8 = sb("top8", [P, TT, 8])
        replaced = sb("replaced", [P, TT, E + TOP])
        chosen = sb("chosen", [P, TT, E])
        wsum = sb("wsum", [P, TT])
        wsum_e = sb("wsum_e", [P, TT])
        winv = sb("winv", [P, TT])
        weight = sb("weight", [P, TT, E])
        w_tok = sb("w_tok", [P, TT, P], F32R)
        wT = {k: sb(f"wT{k}", [P, BLK], F32R) for k in (1, 4)}

        raw_loaded = [sem(f"raw_loaded{n}") for n in range(NBATCH)]
        vec_loaded = sem("vec_loaded")
        pool_const = sem("pool_const")
        dve_const = sem("dve_const")
        a_done = sem("a_done")
        w_transposed = sem("w_transposed")
        w_hi_done = sem("w_hi_done")
        w_lo_done = sem("w_lo_done")
        wb_ready = sem("wb_ready")
        gate_ready = sem("gate_ready")
        up_ready = sem("up_ready")
        silu_done = sem("silu_done")
        weighted_done = sem("weighted_done")
        hid_done = sem("hid_done")
        hid_hi_done = sem("hid_hi_done")
        hid_lo_done = sem("hid_lo_done")
        down_done = sem("down_done")
        ffn_copied = {k: sem(f"ffn_copied{k}") for k in (1, 4)}
        ffn_transposed = {k: sem(f"ffn_transposed{k}") for k in (1, 4)}
        ffn_added = {k: sem(f"ffn_added{k}") for k in (1, 4)}
        ln_stats = {k: sem(f"ln_stats{k}") for k in LN}
        ln_scale = {k: sem(f"ln_scale{k}") for k in LN}
        ln_normed = {k: sem(f"ln_normed{k}") for k in LN}
        xn_transposed = {k: sem(f"xn_transposed{k}") for k in (1, 2, 4)}
        xT_hi_done = {k: sem(f"xT_hi_done{k}") for k in (1, 2, 4)}
        xT_lo_done = {k: sem(f"xT_lo_done{k}") for k in (1, 2, 4)}
        logitsT_ready = {k: sem(f"logitsT_ready{k}") for k in (1, 4)}
        logitsT_copied = {k: sem(f"logitsT_copied{k}") for k in (1, 4)}
        logits_ready = {k: sem(f"logits_ready{k}") for k in (1, 4)}
        logit_silu_done = {k: sem(f"logit_silu_done{k}") for k in (1, 4)}
        route = {k: sem(f"route{k}") for k in (1, 4)}
        route_transposed = {k: sem(f"route_transposed{k}") for k in (1, 4)}
        wT_done = {k: sem(f"wT_done{k}") for k in (1, 4)}
        x_ln_loaded = sem("x_ln_loaded")
        x_res_loaded = sem("x_res_loaded")
        mix_gate_ready = sem("mix_gate_ready")
        mix_gate_done = sem("mix_gate_done")
        mix_val_ready = sem("mix_val_ready")
        mix_val_done = sem("mix_val_done")
        mix = sem("mix")
        y_hi_done = sem("y_hi_done")
        y_lo_done = sem("y_lo_done")
        mix_out_ready = sem("mix_out_ready")
        res_done = sem("res_done")
        x1_b_done = sem("x1_b_done")
        scaled_done = sem("scaled_done")
        x2_done = sem("x2_done")
        x2_kept_done = sem("x2_kept_done")
        stored = sem("stored")

        AT1 = {"mixer out": 0, "mixer sum": 0.5, "stats 3": 1, "norm 3": 2, "normalise 3": 3, "scale 3": 4,
               "x2": 4.5, "stats 4": 5, "norm 4": 5, "normalise 4": 6, "keep x2": 9, "transpose 4": 8,
               "xT high 4": 8, "xT low 4": 8.5, "router": 9, "copy logits": 9, "transpose logits": 10,
               "logits": 10.5, "silu logits": 11, "route": 11.5,
               "copy ffn": 2, "transpose ffn": 4, "add ffn": 6}
        AT2 = {"norm 1": 0, "normalise 1": 0, "transpose 1": 1, "xT high 1": 1, "xT low 1": 1.5,
               "router": 2, "copy logits": 2, "transpose logits": 3, "logits": 3.5, "silu logits": 4, "route": 6,
               "copy ffn": 2, "transpose ffn": 4, "add ffn": 4.5, "stats 2": 5, "norm 2": 5, "normalise 2": 6,
               "add ln_b": 9, "transpose 2": 7, "xT high 2": 7, "xT low 2": 8, "mixer gate": 9, "tanh gate": 9,
               "mixer value": 10, "copy value": 10, "conv": 11, "transpose weights": 13, "copy weights": 13,
               "y high": 14, "y low": 14, "stats 1": 15}
        PARTS = 11

        ROUTE = 32
        LOGITS_READ = 2
        MIX = K + 2

        block = ctx.enter_context(nc.Block())

        setup_banks = [gate_ps[0], gate_ps[1], up_ps[0], up_ps[1]]

        def setup_bank(n):
            return setup_banks[n % len(setup_banks)][:, :]


        def is_block(b, n):
            return isinstance(b, int) and b == n

        def ffns_before(k, b):
            if k == 1:
                return 0 if is_block(b, 0) else b * 2 - 1
            return b * 2 + (1 if is_block(b, NBLK - 1) else 2)

        def first_tile(k, b):
            return ffns_before(k, b) * NT

        def first_pair(k, b):
            return ffns_before(k, b) * NPAIR

        def start_parity(k, b):
            if k == 1:
                return 0 if is_block(b, 0) else NT % 2
            return NT % 2 if is_block(b, NBLK - 1) else 0

        def ring_before(j):
            return RING if j >= RING else j + NT - max(m for m in range(NT) if m % RING == j)

        @block.sync
        def _(sp):
            def load_x_ln(b):
                if not is_block(b, 0):
                    sp.wait_ge(ln_normed[1], b)
                sp.dma_start(x_ln[:, :, :], x_blk[b]).then_inc(x_ln_loaded, 16)

            def load_x_res(b):
                if not is_block(b, 0):
                    sp.wait_ge(ffn_added[1], b)
                sp.dma_start(x_res[:, :, :], x_blk[b]).then_inc(x_res_loaded, 16)

            def store(b):
                sp.wait_ge(ffn_added[4], b + 1)
                sp.dma_start(out_blk[b], x3[:, :, :]).then_inc(stored, 16)

            load_x_ln(0)
            sp.dma_start(raw[:, WIN_G:WOUT, :], W_in.rearrange("(n p) h -> p n h", p=P))\
              .then_inc(raw_loaded[0], 16)
            sp.dma_start(raw[:, WOUT, :], W_out).then_inc(raw_loaded[0], 16)
            sp.wait_ge(dve_const, 1)
            sp.dma_start(raw[0:E, WROUTER, :], router_w).then_inc(raw_loaded[0], 16)
            gate_v = gate_w.rearrange("e i h -> (e i) h").rearrange("(n p) h -> p n h", p=P)
            up_v = up_w.rearrange("e i h -> (e i) h").rearrange("(n p) h -> p n h", p=P)
            down_v = down_w.rearrange("e h i -> h e i")
            for q in range(4):
                for n, (tile, view) in enumerate(((gate_tile, gate_v), (up_tile, up_v))):
                    sp.dma_start(raw[:, tile(4 * q):tile(4 * q) + 4, :], view[:, 4 * q:4 * q + 4, :])\
                      .then_inc(raw_loaded[1 + 3 * q + n], 16)
                dst = raw[:, down_tile(4 * q):down_tile(4 * q) + 4, :]
                sp.dma_start(dst.rearrange("p n (e i) -> p (n e) i", e=2), down_v[:, 8 * q:8 * q + 8, :])\
                  .then_inc(raw_loaded[3 + 3 * q], 16)
            for n, w in enumerate((sh_gate, sh_up, sh_down)):
                sp.dma_start(raw[:, 52 + n, :], w).then_inc(raw_loaded[NBATCH - 1], 16)
            load_x_res(0)
            load_x_ln(1)

            def step(i, first=False):
                load_x_res(i)
                load_x_ln(i + 1)
                store(i - 2)

            load_x_res(1)
            load_x_ln(2)
            with sp.Fori(2, NBLK - 1) as i:
                step(i)
            load_x_res(NBLK - 1)
            for b in range(NBLK - 3, NBLK):
                store(b)
            sp.wait_ge(stored, 16 * NBLK)

        @block.gpsimd
        def _(pool):
            pool.dma_start(bias_b[:, :], router_b.partition_broadcast(P)).then_inc(vec_loaded, 16)
            pool.dma_start(lnw_b[:, :], ln_w.partition_broadcast(P)).then_inc(vec_loaded, 16)
            pool.dma_start(lnb_b[:, :], ln_b.partition_broadcast(P)).then_inc(vec_loaded, 16)
            pool.dma_start(taps[:, :], conv_w.rearrange("d o k -> d (o k)")).then_inc(vec_loaded, 16)
            pool.dma_start(cbias[:, :], conv_b.unsqueeze(1)).then_inc(vec_loaded, 16)
            pool.dma_start(a_raw[:, :], a_param.unsqueeze(1)).then_inc(vec_loaded, 16)
            const = Steps(pool, pool_const, 0)
            const.done(nc.gpsimd.memset(zeros[:, :], 0.0))
            const.done(nc.gpsimd.memset(neg_half[:, :], -0.5))
            const.done(nc.gpsimd.memset(eps[:, :], EPS))
            const.wait()
            const.done(nc.gpsimd.affine_select(out=ident[:, :], in_=zeros[:, :], fill=1.0,
                                               compare_op=ALU.not_equal, base=0,
                                               pattern=[[-1, P]], channel_multiplier=1))
            const.done(nc.gpsimd.affine_select(
                out=beat_at[:, :, :], in_=zeros[:, 0:NG * NG].rearrange("p (g h) -> p g h", g=NG),
                fill=1e-37, compare_op=ALU.is_gt, base=0, pattern=[[1, NG], [-1, NG]], channel_multiplier=0))
            spread = [[-2, NPAIR], [-1, 2], [0, I]]
            as_rows = lambda t: t[:, :, :].rearrange("p n (e i) -> p n e i", e=2)
            const.done(nc.gpsimd.affine_select(out=as_rows(pick_half), in_=zeros[:, :].rearrange("p (e i) -> p e i", e=2).unsqueeze(1)
                                               .broadcast_to([P, NPAIR, 2, I]), fill=1.0,
                                               compare_op=ALU.not_equal, base=0,
                                               pattern=spread, channel_multiplier=1))
            const.wait()
            const.done(nc.gpsimd.affine_select(out=as_rows(pick), in_=as_rows(pick_half), fill=1.0,
                                               compare_op=ALU.not_equal, base=-E,
                                               pattern=spread, channel_multiplier=1))
            assert const.n == 7

            def hidden_low(k, b, j):
                n = first_tile(k, b) + j
                s = j % RING
                pool.wait_ge(hid_hi_done, n + 1)
                nc.gpsimd.tensor_tensor(hid_lo[s][:, :], hid[s][:, :], hid_hi[s][:, :].bitcast(F32),
                                        ALU.subtract).then_inc(hid_lo_done, 1)

            def norm_scale(k, b):
                st = Steps(pool, ln_scale[k], b * 4)
                pool.wait_ge(ln_stats[k], b * 2 + 2)
                st.done(nc.gpsimd.tensor_tensor(neg_mean[k][:, :], zeros[:, 0:TT], meanvar[k][:, :, 0],
                                                ALU.subtract))
                st.done(nc.gpsimd.tensor_tensor(var_eps[k][:, :], meanvar[k][:, :, 1], eps[:, :], ALU.add))
                st.wait()
                st.done(nc.gpsimd.tensor_tensor(rstd[k][:, :], var_eps[k][:, :], neg_half[:, :], ALU.pow))
                st.wait()
                st.done(nc.gpsimd.tensor_tensor(shift[k][:, :], neg_mean[k][:, :], rstd[k][:, :], ALU.mult))

            def ffn1_unit(i, main=True, tail=True):
                for j in range(NT):
                    if tail and j == AT1["norm 3"]:
                        norm_scale(3, i - 1)
                    if tail and j == AT1["norm 4"]:
                        norm_scale(4, i - 1)
                    if main:
                        hidden_low(1, i, j)

            def ffn2_unit(i, main=True, chain=True, prepare=True):
                for j in range(NT):
                    if chain and j == AT2["norm 2"]:
                        norm_scale(2, i)
                    if chain and j == AT2["add ln_b"]:
                        bc = lnb_b[:, :].unsqueeze(1).broadcast_to([P, TT, P])
                        nc.gpsimd.tensor_tensor(x1_b[:, :, :], x1[:, :, :], bc, ALU.add).then_inc(x1_b_done, 1)
                    if chain and j == AT2["y low"]:
                        pool.wait_ge(y_hi_done, i + 1)
                        nc.gpsimd.tensor_tensor(y_lo[:, :], y[:, :], y_hi[:, :].bitcast(F32),
                                                ALU.subtract).then_inc(y_lo_done, 1)
                    if prepare and j == AT2["norm 1"]:
                        norm_scale(1, i + 1)
                    if main:
                        hidden_low(4, i - 1, j)

            norm_scale(1, 0)
            pool.wait_ge(vec_loaded, 16 * 6)
            ffn1_unit(0, tail=False)
            ffn2_unit(0, main=False)
            ffn1_unit(1)
            ffn2_unit(1)
            with pool.Fori(2, NBLK - 1) as i:
                ffn1_unit(i)
                ffn2_unit(i)
            ffn1_unit(NBLK - 1)
            ffn2_unit(NBLK - 1, prepare=False)
            ffn1_unit(NBLK, main=False)
            ffn2_unit(NBLK, chain=False, prepare=False)

        @block.scalar
        def _(act):
            def weight_high(n):
                act.wait_ge(w_transposed, n + 1)
                nc.scalar.activation(wt_hi[:, 4 * n:4 * n + 4, :].rearrange("p n c -> p (n c)"),
                                     setup_bank(n), ACT.Copy).then_inc(w_hi_done, 1)

            def silu_tile(k, b, j):
                n = first_tile(k, b) + j
                s = (start_parity(k, b) + j) % 2
                act.wait_ge(gate_ready, n + 1)
                if not (isinstance(n, int) and n < 2):
                    act.wait_ge(hid_done, n - 1)
                nc.scalar.activation(silu_sb[s][:, :], gate_ps[s][:, :], ACT.Silu).then_inc(silu_done, 1)

            def hidden_high(k, b, j):
                n = first_tile(k, b) + j
                s = j % RING
                act.wait_ge(hid_done, n + 1)
                last = n - ring_before(j)
                if not (isinstance(last, int) and last < 0):
                    act.wait_ge(down_done, last + 1)
                nc.scalar.activation(hid_hi[s][:, :], hid[s][:, :], ACT.Copy).then_inc(hid_hi_done, 1)

            def tile(k, b, j, before):
                silu_tile(k, b, j)
                if j > 0:
                    hidden_high(k, b, j - 1)
                elif before is not None:
                    hidden_high(*before, NT - 1)

            def ffn_copy(k, b):
                act.wait_ge(down_done, first_tile(k, b) + NT)
                nc.scalar.activation(ffn_sb[k][:, :], down_ps[:, :], ACT.Copy).then_inc(ffn_copied[k], 1)

            def xT_high(k, b):
                act.wait_ge(xn_transposed[k], b + 1)
                nc.scalar.activation(xT_hi[k][:, :], side[:, :], ACT.Copy).then_inc(xT_hi_done[k], 1)

            def silu_logits(k, b):
                act.wait_ge(route[k], b * ROUTE + 2)
                nc.scalar.activation(logit_silu[:, :, :], logit[:, :, :], ACT.Silu)\
                  .then_inc(logit_silu_done[k], 1)

            def wT_copy(k, b):
                act.wait_ge(route_transposed[k], b + 1)
                nc.scalar.activation(wT[k][:, :], side[:, :], ACT.Copy).then_inc(wT_done[k], 1)

            def normalise(k, b, src):
                act.wait_ge(ln_scale[k], b * 4 + 4)
                for t in range(TT):
                    last = nc.scalar.activation(normed[k][:, t, :], src[:, t, :], ACT.Identity,
                                                bias=shift[k][:, t:t + 1], scale=rstd[k][:, t:t + 1])
                last.then_inc(ln_normed[k], 1)

            def copy_logits(k, b):
                act.wait_ge(logitsT_ready[k], b + 1)
                nc.scalar.activation(logitsT[:, :], side[:, :], ACT.Copy).then_inc(logitsT_copied[k], 1)

            def ffn1_unit(i, main=True, tail=True, output=True):
                before = (4, i - 2) if output else None
                for j in range(NT):
                    if main:
                        tile(1, i, j, before)
                    if output and j == AT1["copy ffn"]:
                        ffn_copy(4, i - 2)
                    if tail and j == AT1["normalise 3"]:
                        normalise(3, i - 1, res)
                    if tail and j == AT1["normalise 4"]:
                        normalise(4, i - 1, x2)
                    if tail and j == AT1["keep x2"]:
                        if output:
                            act.wait_ge(ffn_added[4], i - 1)
                        nc.scalar.activation(x2_kept[:, :, :], x2[:, :, :], ACT.Copy).then_inc(x2_kept_done, 1)
                    if tail and j == AT1["xT high 4"]:
                        xT_high(4, i - 1)
                    if tail and j == AT1["copy logits"]:
                        copy_logits(4, i - 1)
                    if tail and j == AT1["silu logits"]:
                        silu_logits(4, i - 1)

            def ffn2_unit(i, main=True, chain=True, prepare=True):
                for j in range(NT):
                    if main:
                        tile(4, i - 1, j, (1, i) if chain else None)
                        if j == 0:
                            wT_copy(4, i - 1)
                    elif j == 0:
                        hidden_high(1, i, NT - 1)
                    if prepare and j == AT2["normalise 1"]:
                        normalise(1, i + 1, x_ln)
                    if prepare and j == AT2["xT high 1"]:
                        xT_high(1, i + 1)
                    if chain and j == AT2["copy ffn"]:
                        ffn_copy(1, i)
                    if prepare and j == AT2["copy logits"]:
                        copy_logits(1, i + 1)
                    if prepare and j == AT2["silu logits"]:
                        silu_logits(1, i + 1)
                    if chain and j == AT2["normalise 2"]:
                        normalise(2, i, x1)
                    if chain and j == AT2["xT high 2"]:
                        xT_high(2, i)
                    if chain and j == AT2["tanh gate"]:
                        act.wait_ge(mix_gate_ready, i + 1)
                        nc.scalar.activation(gate_t[:, :], side[:, :], ACT.Tanh, scale=0.5)\
                          .then_inc(mix_gate_done, 1)
                    if chain and j == AT2["copy value"]:
                        act.wait_ge(mix_val_ready, i + 1)
                        nc.scalar.activation(val_pad[:, :, PADK:PADK + SEQ],
                                             side[:, :].rearrange("p (s t) -> p s t", s=SB), ACT.Copy)\
                          .then_inc(mix_val_done, 1)
                    if prepare and j == AT2["copy weights"]:
                        wT_copy(1, i + 1)
                    if chain and j == AT2["y high"]:
                        act.wait_ge(mix, i * MIX + MIX)
                        nc.scalar.activation(y_hi[:, :], y[:, :], ACT.Copy).then_inc(y_hi_done, 1)

            act.wait_ge(vec_loaded, 16 * 6)
            nc.scalar.activation(a_tanh[:, :], a_raw[:, :], ACT.Tanh).then_inc(a_done, 1)
            for n in range(NBATCH):
                weight_high(n)
                if n == 0:
                    normalise(1, 0, x_ln)
                if n == 1:
                    xT_high(1, 0)
                if n == 2:
                    copy_logits(1, 0)
                if n == 4:
                    silu_logits(1, 0)
            wT_copy(1, 0)
            ffn1_unit(0, tail=False, output=False)
            ffn2_unit(0, main=False)
            ffn1_unit(1, output=False)
            ffn2_unit(1)
            with act.Fori(2, NBLK - 1) as i:
                ffn1_unit(i)
                ffn2_unit(i)
            ffn1_unit(NBLK - 1)
            ffn2_unit(NBLK - 1, prepare=False)
            hidden_high(4, NBLK - 2, NT - 1)
            ffn1_unit(NBLK, main=False)
            ffn2_unit(NBLK, chain=False, prepare=False)
            hidden_high(4, NBLK - 1, NT - 1)
            ffn_copy(4, NBLK - 1)

        @block.vector
        def _(dve):
            V = nc.vector

            def weight_low(n):
                dve.wait_ge(w_hi_done, n + 1)
                V.tensor_tensor(wt_lo[:, 4 * n:4 * n + 4, :].rearrange("p n c -> p (n c)"), setup_bank(n),
                                wt_hi[:, 4 * n:4 * n + 4, :].rearrange("p n c -> p (n c)").bitcast(F32),
                                ALU.subtract).then_inc(w_lo_done, 1)

            def weigh_tile(k, b, j):
                n = first_tile(k, b) + j
                s = (start_parity(k, b) + j) % 2
                dve.wait_ge(silu_done, n + 1)
                dve.wait_ge(wb_ready, first_pair(k, b) + j + 1)
                V.tensor_tensor(weighted[s][:, :], silu_sb[s][:, :], wb_ps[j % 2][:, :], ALU.mult)\
                 .then_inc(weighted_done, 1)

            def hidden_tile(k, b, j):
                n = first_tile(k, b) + j
                s = (start_parity(k, b) + j) % 2
                dve.wait_ge(up_ready, n + 1)
                if j < NPAIR:
                    dve.wait_ge(weighted_done, first_pair(k, b) + j + 1)
                else:
                    dve.wait_ge(silu_done, n + 1)
                last = n - ring_before(j)
                if not (isinstance(last, int) and last < 0):
                    dve.wait_ge(hid_lo_done, last + 1)
                factor = weighted[s] if j < NPAIR else silu_sb[s]
                V.tensor_tensor(hid[j % RING][:, :], factor[:, :], up_ps[s][:, :], ALU.mult).then_inc(hid_done, 1)

            def norm_stats(k, b, src):
                for t in range(TT):
                    last = V.bn_stats(stats[k][:, t, :], src[:, t, :])
                last.then_inc(ln_stats[k], 1)
                dve.wait_ge(ln_stats[k], b * 2 + 1)
                V.memset(hold[:, :], 0.0)
                for t in range(TT):
                    last = V.bn_aggr(meanvar[k][:, t, :], stats[k][:, t, :])
                last.then_inc(ln_stats[k], 1)

            def xT_low(k, b):
                dve.wait_ge(xT_hi_done[k], b + 1)
                V.tensor_tensor(xT_lo[k][:, :], side[:, :], xT_hi[k][:, :].bitcast(F32), ALU.subtract)\
                 .then_inc(xT_lo_done[k], 1)

            def route_logits(k, b, st):
                dve.wait_ge(logits_ready[k], b + 1)
                st.done(V.tensor_scalar(tiny[:, :, :], side_te, -1e-9, 1e-8, ALU.is_ge, ALU.mult))
                st.wait()
                st.done(V.tensor_tensor(logit[:, :, :], tiny[:, :, :], side_te, ALU.add))
                st.wait()
                st.done(V.reciprocal(logit_inv[:, :, :], logit[:, :, :]))

            def route_part(k, b, st, part):
                if part == 0:
                    dve.wait_ge(logit_silu_done[k], b + 1)
                    st.wait()
                    st.done(V.tensor_tensor(score[:, :, :], logit_silu[:, :, :], logit_inv[:, :, :], ALU.mult))
                    st.wait()
                    st.done(V.tensor_tensor(biased[:, :, :], score[:, :, :],
                                            bias_b[:, :].unsqueeze(1).broadcast_to([P, TT, E]), ALU.add))
                if part == 1:
                    st.wait()
                    g8 = biased[:, :, :].rearrange("p t (g c) -> p (t g) c", g=NG)
                    st.done(V.tensor_tensor(hi4[:, :, :], g8[:, :, 0:4], g8[:, :, 4:8], ALU.max))
                    st.done(V.tensor_tensor(lo4[:, :, :], g8[:, :, 0:4], g8[:, :, 4:8], ALU.min))
                    st.wait()
                    st.done(V.tensor_tensor(hi2[:, :, :], hi4[:, :, 0:2], hi4[:, :, 2:4], ALU.max))
                    st.done(V.tensor_tensor(lo2a[:, :, :], hi4[:, :, 0:2], hi4[:, :, 2:4], ALU.min))
                    st.done(V.tensor_tensor(lo2b[:, :, :], lo4[:, :, 0:2], lo4[:, :, 2:4], ALU.max))
                if part == 2:
                    st.wait()
                    st.done(V.tensor_tensor(lo2[:, :, :], lo2a[:, :, :], lo2b[:, :, :], ALU.max))
                    st.done(V.tensor_tensor(hi1[:, :, :], hi2[:, :, 0:1], hi2[:, :, 1:2], ALU.max))
                    st.done(V.tensor_tensor(lo1a[:, :, :], hi2[:, :, 0:1], hi2[:, :, 1:2], ALU.min))
                    st.wait()
                    st.done(V.tensor_tensor(lo1b[:, :, :], lo2[:, :, 0:1], lo2[:, :, 1:2], ALU.max))
                if part == 3:
                    st.wait()
                    st.done(V.tensor_tensor(lo1[:, :, :], lo1a[:, :, :], lo1b[:, :, :], ALU.max))
                    st.wait()
                    st.done(V.tensor_tensor(gsum[:, :, :].rearrange("p t g -> p (t g)").unsqueeze(2),
                                            hi1[:, :, :], lo1[:, :, :], ALU.add))
                if part == 4:
                    st.wait()
                    for t in range(TT):
                        last = V.tensor_tensor(gdiff[:, t, :].rearrange("p (g h) -> p g h", g=NG),
                                               gsum[:, t, :].unsqueeze(1).broadcast_to([P, NG, NG]),
                                               gsum[:, t, :].unsqueeze(2).broadcast_to([P, NG, NG]), ALU.subtract)
                    st.done(last)
                    st.wait()
                    st.done(V.tensor_tensor(beats[:, :, :].rearrange("p (t g) h -> p t (g h)", t=TT), gdiff[:, :, :],
                                            beat_at[:, :, :].rearrange("p g h -> p (g h)").unsqueeze(1)
                                            .broadcast_to([P, TT, NG * NG]), ALU.is_ge))
                if part == 5:
                    st.wait()
                    st.done(V.tensor_reduce(grank[:, :], beats[:, :, :], AX.X, ALU.add))
                    st.wait()
                    st.done(V.tensor_scalar(gmask[:, :], grank[:, :], float(GTOP), None, ALU.is_lt))
                if part == 6:
                    st.wait()
                    st.done(V.tensor_tensor(masked0[:, :, :].rearrange("p t (g c) -> p (t g) c", g=NG),
                                            biased[:, :, :].rearrange("p t (g c) -> p (t g) c", g=NG),
                                            gmask[:, :].unsqueeze(2).broadcast_to([P, TT * NG, PG]), ALU.mult))
                    st.wait()
                    st.done(V.tensor_scalar(masked[:, :, 0:E], masked0[:, :, :], 0.0, None, ALU.add))
                if part == 7:
                    st.wait()
                    V.memset(hold[:, :], 0.0)
                    for t in range(TT):
                        last = V.max(top8[:, t, :], masked[:, t, 0:E])
                    st.done(last)
                if part == 8:
                    st.wait()
                    st.done(V.memset(top8[:, :, TOP:8], FAR))
                    st.wait()
                    V.memset(hold[:, :], 0.0)
                    for t in range(TT):
                        last = V.match_replace(replaced[:, t, :], top8[:, t, :], masked[:, t, :], GONE)
                    st.done(last)
                if part == 9:
                    st.wait()
                    st.done(V.scalar_tensor_tensor(chosen[:, :, :], replaced[:, :, 0:E], (FAR + GONE) / 2,
                                                   score[:, :, :], ALU.is_lt, ALU.mult))
                    st.wait()
                    st.done(V.tensor_reduce(wsum[:, :], chosen[:, :, :], AX.X, ALU.add))
                    st.wait()
                    st.done(V.tensor_scalar(wsum_e[:, :], wsum[:, :], 1e-20, None, ALU.add))
                if part == 10:
                    st.wait()
                    st.done(V.reciprocal(winv[:, :], wsum_e[:, :]))
                    st.wait()
                    st.done(V.scalar_tensor_tensor(weight[:, :, :], chosen[:, :, :], SCALE,
                                                   winv[:, :].unsqueeze(2).broadcast_to([P, TT, E]),
                                                   ALU.mult, ALU.mult))
                    st.wait()
                    st.done(V.tensor_copy(w_tok[:, :, 0:E], weight[:, :, :]))
                    st.wait()
                    st.done(V.tensor_tensor(w_tok[:, :, E:2 * E], weight[:, :, :], w_tok[:, :, 0:E].bitcast(F32),
                                            ALU.subtract))
                    assert st.n == ROUTE

            def conv_tap(i, st, t):
                src = val_pad[:, :, t:t + SEQ]
                if t == 0:
                    dve.wait_ge(mix_val_done, i + 1)
                    st.done(V.tensor_scalar(conv[0][:, :, :], src, taps_half[:, 0:1], cbias_half[:, 0:1],
                                            ALU.mult, ALU.add))
                else:
                    st.wait()
                    st.done(V.scalar_tensor_tensor(conv[t % 2][:, :, :], src, taps_half[:, t:t + 1],
                                                   conv[(t + 1) % 2][:, :, :], ALU.mult, ALU.add))

            def gate_value(i, st):
                dve.wait_ge(mix_gate_done, i + 1)
                st.wait()
                st.done(V.scalar_tensor_tensor(gated[:, :].rearrange("p (s t) -> p s t", s=SB),
                                               gate_t[:, :].rearrange("p (s t) -> p s t", s=SB), 1.0,
                                               conv[(K - 1) % 2][:, :, :], ALU.add, ALU.mult))

            def recur(i, st):
                st.wait()
                if not is_block(i, 0):
                    dve.wait_ge(y_lo_done, i)
                st.done(V.tensor_tensor_scan(y[:, :], decay[:, :], gated[:, :], 0.0, ALU.mult, ALU.add))
                assert st.n == MIX

            def ffn_add(k, b, residual, dst):
                dve.wait_ge(ffn_transposed[k], b + 1)
                V.scalar_tensor_tensor(dst[:, :, :], side_td, 0.5, residual[:, :, :], ALU.mult, ALU.add)\
                 .then_inc(ffn_added[k], 1)

            def beside_ffn1(i, at, st, tail, output):
                if tail and at == AT1["mixer sum"]:
                    dve.wait_ge(mix_out_ready, i)
                    V.tensor_tensor(res[:, :, :], side_td, normed[2][:, :, :], ALU.add).then_inc(res_done, 1)
                if tail and at == AT1["stats 3"]:
                    dve.wait_ge(res_done, i)
                    norm_stats(3, i - 1, res)
                if tail and at == AT1["scale 3"]:
                    dve.wait_ge(ln_normed[3], i)
                    V.tensor_tensor(scaled[:, :, :], normed[3][:, :, :],
                                    lnw_b[:, :].unsqueeze(1).broadcast_to([P, TT, P]), ALU.mult)\
                     .then_inc(scaled_done, 1)
                if tail and at == AT1["x2"]:
                    dve.wait_ge(x1_b_done, i)
                    dve.wait_ge(scaled_done, i)
                    if not is_block(i, 1):
                        dve.wait_ge(x2_kept_done, i - 1)
                    V.tensor_tensor(x2[:, :, :], scaled[:, :, :], x1_b[:, :, :], ALU.add).then_inc(x2_done, 1)
                if tail and at == AT1["stats 4"]:
                    dve.wait_ge(x2_done, i)
                    norm_stats(4, i - 1, x2)
                if output and at == AT1["add ffn"]:
                    if not is_block(i, 2):
                        dve.wait_ge(stored, (i - 2) * 16)
                    ffn_add(4, i - 2, x2_kept, x3)
                if tail and at == AT1["xT low 4"]:
                    xT_low(4, i - 1)
                if tail and at == AT1["logits"]:
                    route_logits(4, i - 1, st)
                for part in range(PARTS):
                    if tail and at == AT1["route"] + part / 2:
                        route_part(4, i - 1, st, part)

            def beside_ffn2(i, at, st, mx, chain, prepare):
                if prepare and at == AT2["xT low 1"]:
                    xT_low(1, i + 1)
                if prepare and at == AT2["logits"]:
                    route_logits(1, i + 1, st)
                if chain and at == AT2["add ffn"]:
                    dve.wait_ge(x_res_loaded, i * 16 + 16)
                    ffn_add(1, i, x_res, x1)
                if chain and at == AT2["stats 2"]:
                    dve.wait_ge(ffn_added[1], i + 1)
                    norm_stats(2, i, x1)
                for part in range(PARTS):
                    if prepare and at == AT2["route"] + part / 2:
                        route_part(1, i + 1, st, part)
                if chain and at == AT2["xT low 2"]:
                    xT_low(2, i)
                for t in range(K):
                    if chain and at == AT2["conv"] + t / 2:
                        conv_tap(i, mx, t)
                if chain and at == AT2["conv"] + K / 2:
                    gate_value(i, mx)
                if chain and at == AT2["conv"] + (K + 1) / 2:
                    recur(i, mx)
                if chain and at == AT2["stats 1"] and not (isinstance(i, int) and i > NBLK - 3):
                    dve.wait_ge(x_ln_loaded, i * 16 + 48)
                    norm_stats(1, i + 2, x_ln)

            def ffn1_unit(i, main=True, tail=True, output=True):
                st = Steps(dve, route[4], (i - 1) * ROUTE) if tail else None
                for j in range(NT):
                    if main and j < NPAIR:
                        weigh_tile(1, i, j)
                    beside_ffn1(i, j, st, tail, output)
                    if main:
                        hidden_tile(1, i, j)
                    beside_ffn1(i, j + 0.5, st, tail, output)

            def ffn2_unit(i, main=True, chain=True, prepare=True):
                st = Steps(dve, route[1], (i + 1) * ROUTE) if prepare else None
                mx = Steps(dve, mix, i * MIX) if chain else None
                for j in range(NT):
                    if main and j < NPAIR:
                        weigh_tile(4, i - 1, j)
                    beside_ffn2(i, j, st, mx, chain, prepare)
                    if main:
                        hidden_tile(4, i - 1, j)
                    beside_ffn2(i, j + 0.5, st, mx, chain, prepare)

            const = Steps(dve, dve_const, 0)
            const.done(V.memset(raw[:, WROUTER, :], 0.0))
            const.done(V.memset(val_pad[:, :, :], 0.0))
            const.done(V.memset(masked[:, :, :], FAR))
            const.done(V.memset(ones[:, :], 1.0))
            const.done(V.memset(w_tok[:, :, :].bitcast(F32), 0.0))
            dve.wait_ge(x_ln_loaded, 16)
            norm_stats(1, 0, x_ln)
            dve.wait_ge(vec_loaded, 16 * 6)
            const.done(V.tensor_scalar(taps_half[:, :], taps[:, :], 0.5, None, ALU.mult))
            const.done(V.tensor_scalar(cbias_half[:, :], cbias[:, :], 0.5, None, ALU.mult))
            dve.wait_ge(a_done, 1)
            const.wait()
            const.done(V.tensor_scalar(decay[:, :], ones[:, :], a_tanh[:, 0:1], None, ALU.mult))
            const.wait()
            const.done(V.memset(decay[:, :].rearrange("p (s t) -> p s t", s=SB)[:, :, 0:1], 0.0))
            const.wait()
            first = Steps(dve, route[1], 0)
            for n in range(NBATCH):
                weight_low(n)
                if n == 1:
                    xT_low(1, 0)
                if n == 3:
                    route_logits(1, 0, first)
                if n == 4:
                    for part in range(PARTS):
                        route_part(1, 0, first, part)
            dve.wait_ge(x_ln_loaded, 32)
            norm_stats(1, 1, x_ln)
            ffn1_unit(0, tail=False, output=False)
            ffn2_unit(0, main=False)
            ffn1_unit(1, output=False)
            ffn2_unit(1)
            with dve.Fori(2, NBLK - 2) as i:
                ffn1_unit(i)
                ffn2_unit(i)
            ffn1_unit(NBLK - 2)
            ffn2_unit(NBLK - 2)
            ffn1_unit(NBLK - 1)
            ffn2_unit(NBLK - 1, prepare=False)
            ffn1_unit(NBLK, main=False)
            ffn2_unit(NBLK, chain=False, prepare=False)
            dve.wait_ge(stored, 16 * (NBLK - 1))
            ffn_add(4, NBLK - 1, x2_kept, x3)

        @block.tensor
        def _(pe):
            def product(dst, w, moving_hi, moving_lo, w_lo, start, stop):
                nc.tensor.matmul(dst, w, moving_hi, start=start, stop=False)
                nc.tensor.matmul(dst, w, moving_lo, start=False, stop=False)
                return nc.tensor.matmul(dst, w_lo, moving_hi, start=False, stop=stop)

            def weights(n):
                pe.wait_ge(raw_loaded[n], {0: 48, NBATCH - 1: 48}.get(n, 16))
                if n >= len(setup_banks):
                    pe.wait_ge(w_lo_done, n - len(setup_banks) + 1)
                for t in range(4):
                    if 4 * n + t <= down_tile(NPAIR):
                        last = nc.tensor.transpose(setup_bank(n)[:, t * P:(t + 1) * P], raw[:, 4 * n + t, :],
                                                   ident[:, :])
                    else:
                        last = nc.tensor.transpose(setup_bank(n)[:, t * P:(t + 1) * P], raw[:, WROUTER, :],
                                                   ident[:, :])
                last.then_inc(w_transposed, 1)

            def spread_weights(k, b, j):
                r = first_pair(k, b) + j
                if not (isinstance(r, int) and r < 2):
                    pe.wait_ge(weighted_done, r - 1)
                nc.tensor.matmul(wb_ps[j % 2][:, :], pick[:, j, :], wT[k][:, :], start=True, stop=True)\
                  .then_inc(wb_ready, 1)

            def up_tiles(k, b, j):
                n = first_tile(k, b) + j
                s = (start_parity(k, b) + j) % 2
                late = not (isinstance(n, int) and n < 2)
                if late:
                    pe.wait_ge(silu_done, n - 1)
                g, u = gate_tile(j), up_tile(j)
                product(gate_ps[s][:, :], wt_hi[:, g, :], xT_hi[k][:, :], xT_lo[k][:, :], wt_lo[:, g, :],
                        True, True).then_inc(gate_ready, 1)
                if j == 1:
                    pe.wait_ge(wT_done[k], b + 1)
                    spread_weights(k, b, 0)
                if 0 < j < NPAIR:
                    spread_weights(k, b, j)
                if late:
                    pe.wait_ge(hid_done, n - 1)
                product(up_ps[s][:, :], wt_hi[:, u, :], xT_hi[k][:, :], xT_lo[k][:, :], wt_lo[:, u, :],
                        True, True).then_inc(up_ready, 1)

            def down(k, b, j):
                n = first_tile(k, b) + j
                s = j % RING
                w = down_tile(j)
                if j == 0:
                    if k == 4:
                        pe.wait_ge(ffn_copied[1], b + 2 if not is_block(b, NBLK - 1) else b + 1)
                    elif not is_block(b, 0):
                        if is_block(b, 1):
                            pe.wait_ge(ffn_copied[1], 1)
                        else:
                            pe.wait_ge(ffn_copied[4], b - 1)
                pe.wait_ge(hid_hi_done, n + 1)
                nc.tensor.matmul(down_ps[:, :], wt_hi[:, w, :], hid_hi[s][:, :], start=(j == 0), stop=False)
                nc.tensor.matmul(down_ps[:, :], wt_lo[:, w, :], hid_hi[s][:, :], start=False, stop=False)
                pe.wait_ge(hid_lo_done, n + 1)
                nc.tensor.matmul(down_ps[:, :], wt_hi[:, w, :], hid_lo[s][:, :], start=False,
                                 stop=(j == NT - 1)).then_inc(down_done, 1)

            def transpose4(src, done):
                for t in range(TT):
                    last = nc.tensor.transpose(side[:, t * P:(t + 1) * P], src(t), ident[:, :])
                last.then_inc(done, 1)

            def transpose_norm(k, b):
                pe.wait_ge(ln_normed[k], b + 1)
                transpose4(lambda t: normed[k][:, t, :], xn_transposed[k])

            def transpose_ffn(k, b):
                pe.wait_ge(ffn_copied[k], b + 1)
                transpose4(lambda t: ffn_sb[k][:, t * P:(t + 1) * P], ffn_transposed[k])

            def router(k, b):
                pe.wait_ge(xT_lo_done[k], b + 1)
                product(side[:, :], wt_hi[:, WROUTER, :], xT_hi[k][:, :], xT_lo[k][:, :], wt_lo[:, WROUTER, :],
                        True, True).then_inc(logitsT_ready[k], 1)

            def transpose_logits(k, b):
                pe.wait_ge(logitsT_copied[k], b + 1)
                transpose4(lambda t: logitsT[:, t * P:(t + 1) * P], logits_ready[k])

            def transpose_route(k, b):
                pe.wait_ge(route[k], b * ROUTE + ROUTE)
                transpose4(lambda t: w_tok[:, t, :].bitcast(F32), route_transposed[k])

            def mixer_out(b):
                for t in range(TT):
                    rows = slice(t * P, (t + 1) * P)
                    nc.tensor.matmul(side[:, rows], y_hi[:, rows], wt_hi[:, WOUT, :], start=True, stop=False)
                    nc.tensor.matmul(side[:, rows], y_hi[:, rows], wt_lo[:, WOUT, :], start=False, stop=False)
                    last = nc.tensor.matmul(side[:, rows], y_lo[:, rows], wt_hi[:, WOUT, :],
                                            start=False, stop=True)
                last.then_inc(mix_out_ready, 1)


            def ffn1_unit(i, main=True, tail=True, output=True):
                if main:
                    pe.wait_ge(xT_lo_done[1], i + 1)
                for j in range(NT):
                    if main:
                        up_tiles(1, i, j)
                        if j >= LAG:
                            down(1, i, j - LAG)
                        elif output:
                            down(4, i - 2, NT - LAG + j)
                    if tail and j == AT1["mixer out"]:
                        if is_block(i, NBLK):
                            pe.wait_ge(mix_val_done, i)
                        else:
                            pe.wait_ge(wT_done[1], i + 1)
                        pe.wait_ge(y_lo_done, i)
                        mixer_out(i - 1)
                    if output and j == AT1["transpose ffn"]:
                        pe.wait_ge(res_done, i)
                        transpose_ffn(4, i - 2)
                    if tail and j == AT1["transpose 4"]:
                        if output:
                            pe.wait_ge(ffn_added[4], i - 1)
                        else:
                            pe.wait_ge(res_done, i)
                        transpose_norm(4, i - 1)
                    if tail and j == AT1["router"]:
                        router(4, i - 1)
                    if tail and j == AT1["transpose logits"]:
                        transpose_logits(4, i - 1)

            def ffn2_unit(i, main=True, chain=True, prepare=True):
                if main:
                    pe.wait_ge(xT_lo_done[4], i)
                for j in range(NT):
                    if main:
                        up_tiles(4, i - 1, j)
                        if j >= LAG:
                            down(4, i - 1, j - LAG)
                        elif chain:
                            down(1, i, NT - LAG + j)
                    elif j < LAG:
                        down(1, i, NT - LAG + j)
                    if main and j == 0:
                        transpose_route(4, i - 1)
                    if prepare and j == AT2["transpose 1"]:
                        if main:
                            pe.wait_ge(wT_done[4], i)
                        else:
                            pe.wait_ge(wT_done[1], 1)
                        transpose_norm(1, i + 1)
                    if prepare and j == AT2["router"]:
                        router(1, i + 1)
                    if prepare and j == AT2["transpose logits"]:
                        transpose_logits(1, i + 1)
                    if chain and j == AT2["transpose ffn"]:
                        if prepare:
                            pe.wait_ge(route[1], (i + 1) * ROUTE + LOGITS_READ)
                        else:
                            pe.wait_ge(wT_done[4], i)
                        transpose_ffn(1, i)
                    if chain and j == AT2["transpose 2"]:
                        pe.wait_ge(ffn_added[1], i + 1)
                        transpose_norm(2, i)
                    if chain and j == AT2["mixer gate"]:
                        pe.wait_ge(xT_lo_done[2], i + 1)
                        product(side[:, :], wt_hi[:, WIN_G, :], xT_hi[2][:, :], xT_lo[2][:, :], wt_lo[:, WIN_G, :],
                                True, True).then_inc(mix_gate_ready, 1)
                    if chain and j == AT2["mixer value"]:
                        pe.wait_ge(mix_gate_done, i + 1)
                        product(side[:, :], wt_hi[:, WIN_V, :], xT_hi[2][:, :], xT_lo[2][:, :], wt_lo[:, WIN_V, :],
                                True, True).then_inc(mix_val_ready, 1)
                    if prepare and j == AT2["transpose weights"]:
                        pe.wait_ge(mix_val_done, i + 1)
                        transpose_route(1, i + 1)

            pe.wait_ge(pool_const, 7)
            pe.wait_ge(dve_const, 5)
            weights(0)
            weights(1)
            transpose_norm(1, 0)
            weights(2)
            pe.wait_ge(w_lo_done, 1)
            router(1, 0)
            weights(3)
            transpose_logits(1, 0)
            for n in range(4, NBATCH):
                weights(n)
            transpose_route(1, 0)
            pe.wait_ge(w_lo_done, NBATCH)
            ffn1_unit(0, tail=False, output=False)
            ffn2_unit(0, main=False)
            ffn1_unit(1, output=False)
            ffn2_unit(1)
            with pe.Fori(2, NBLK - 1) as i:
                ffn1_unit(i)
                ffn2_unit(i)
            ffn1_unit(NBLK - 1)
            ffn2_unit(NBLK - 1, prepare=False)
            for j in range(NT - LAG, NT):
                down(4, NBLK - 2, j)
            ffn1_unit(NBLK, main=False)
            ffn2_unit(NBLK, chain=False, prepare=False)
            for j in range(NT - LAG, NT):
                down(4, NBLK - 1, j)
            pe.wait_ge(ffn_added[4], NBLK - 1)
            transpose_ffn(4, NBLK - 1)


_INS = ["L0_attn_x", "L0_attn_W_in", "L0_attn_conv_w", "L0_attn_conv_b", "L0_attn_a_param", "L0_attn_W_out",
        "L0_attn_ln_w", "L0_attn_ln_b", "L0_ffn_router_weight", "L0_ffn_router_bias", "L0_ffn_gate_w",
        "L0_ffn_up_w", "L0_ffn_down_w", "L0_ffn_shared_gate_w", "L0_ffn_shared_up_w", "L0_ffn_shared_down_w"]


def kernel(**inputs):
    import numpy as np
    import concourse.bacc as bacc
    from concourse.bass_utils import run_bass_kernel_spmd

    nc = bacc.Bacc("TRN2", target_bir_lowering=False, num_devices=1)
    arrays, args = {}, []
    for name in _INS:
        a = np.ascontiguousarray(inputs[name])
        arrays[f"in_{name}"] = a
        args.append(nc.dram_tensor(f"in_{name}", a.shape, mybir.dt.from_np(a.dtype), kind="ExternalInput").ap())
    shape = arrays["in_L0_attn_x"].shape
    out = nc.dram_tensor("out_x", shape, F32, kind="ExternalOutput").ap()
    macaron_kernel(nc, *args, out)
    r = run_bass_kernel_spmd(nc, [arrays], core_ids=[0])
    return r.results[0]["out_x"]
```

```python
from contextlib import ExitStack

import concourse.bass as bass
from concourse import mybir

F32 = mybir.dt.float32
F32R = mybir.dt.float32r
ALU = mybir.AluOpType
ACT = mybir.ActivationFunctionType
AX = mybir.AxisListType

P = 128
SEQS, SEQ = 16, 256
BLK = 512
NBLK = SEQS * SEQ // BLK
TT = BLK // P
SB = BLK // SEQ
E, I = 32, 64
NPAIR = E * I // P
NT = NPAIR + 1
NG, PG = 4, E // 4
GTOP, TOP = 2, 4
SCALE = 2.5
K = 5
PADK = K // 2
EPS = 1e-5
FAR, GONE = -2.0e38, -3.0e38
LAG = 3
RING = 3
NBATCH = 14


def gate_tile(j):
    return 4 + 12 * (j // 4) + j % 4 if j < NPAIR else 52


def up_tile(j):
    return gate_tile(j) + (4 if j < NPAIR else 1)


def down_tile(j):
    return gate_tile(j) + (8 if j < NPAIR else 2)


WIN_G, WIN_V, WOUT, WROUTER = 0, 1, 2, 3


class Steps:

    def __init__(self, engine, sem, base):
        self.engine, self.sem, self.base, self.n = engine, sem, base, 0

    def done(self, instruction):
        instruction.then_inc(self.sem, 1)
        self.n += 1

    def wait(self):
        self.engine.wait_ge(self.sem, self.base + self.n)


def macaron_kernel(nc, x, W_in, conv_w, conv_b, a_param, W_out, ln_w, ln_b, router_w, router_b,
                   gate_w, up_w, down_w, sh_gate, sh_up, sh_down, out):
    x_blk = x.rearrange("a s d -> (a s) d").rearrange("(n t p) d -> n p t d", t=TT, p=P)
    out_blk = out.rearrange("a s d -> (a s) d").rearrange("(n t p) d -> n p t d", t=TT, p=P)

    with ExitStack() as ctx:
        def is_block(b, n):
            return isinstance(b, int) and b == n

        def sb(name, shape, dt=F32):
            return ctx.enter_context(nc.sbuf_tensor(name, shape, dt))

        def psum(name):
            return ctx.enter_context(nc.psum_tensor(name, [P, BLK], F32))

        def sem(name):
            return ctx.enter_context(nc.semaphore(name))

        gate_ps = [psum("gate_ps0"), psum("gate_ps1")]
        up_ps = [psum("up_ps0"), psum("up_ps1")]
        wb_ps = [psum("wb_ps0"), psum("wb_ps1")]
        down_ps = psum("down_ps")
        side = psum("side")
        side_td = side[:, :].rearrange("p (t d) -> p t d", t=TT)
        side_te = side_td[:, :, 0:E]

        raw = sb("raw", [P, NBATCH * 4, P])
        wt_hi = sb("wt_hi", [P, NBATCH * 4, P], F32R)
        wt_lo = sb("wt_lo", [P, NBATCH * 4, P], F32R)
        ident = sb("ident", [P, P])
        zeros = sb("zeros", [P, P])
        pick = sb("pick", [P, NPAIR, P], F32R)
        neg_half = sb("neg_half", [P, TT])
        eps = sb("eps", [P, TT])
        hold = sb("hold", [P, 1])
        beat_at = sb("beat_at", [P, NG, NG])
        bias_b = sb("bias_b", [P, E])
        lnw_b = sb("lnw_b", [P, P])
        lnb_b = sb("lnb_b", [P, P])
        taps = sb("taps", [P, K])
        taps_half = sb("taps_half", [P, K])
        cbias = sb("cbias", [P, 1])
        cbias_half = sb("cbias_half", [P, 1])
        a_raw = sb("a_raw", [P, 1])
        a_tanh = sb("a_tanh", [P, 1])
        ones = sb("ones", [P, BLK])
        decay = sb("decay", [P, BLK])
        silu_sb = [sb("silu_sb0", [P, BLK]), sb("silu_sb1", [P, BLK])]
        weighted = [sb("weighted0", [P, BLK]), sb("weighted1", [P, BLK])]
        hid = [sb(f"hid{n}", [P, BLK]) for n in range(RING)]
        hid_hi = [sb(f"hid_hi{n}", [P, BLK], F32R) for n in range(RING)]
        hid_lo = [sb(f"hid_lo{n}", [P, BLK], F32R) for n in range(RING)]
        LN = (1, 2, 3, 4)
        stats = {k: sb(f"stats{k}", [P, TT, 6]) for k in LN}
        meanvar = {k: sb(f"meanvar{k}", [P, TT, 2]) for k in LN}
        var_eps = {k: sb(f"var_eps{k}", [P, TT]) for k in LN}
        neg_mean = {k: sb(f"neg_mean{k}", [P, TT]) for k in LN}
        shift = {k: sb(f"shift{k}", [P, TT]) for k in LN}
        rstd = {k: sb(f"rstd{k}", [P, TT]) for k in LN}
        normed = {k: sb(f"normed{k}", [P, TT, P]) for k in LN}
        xT_hi = {k: sb(f"xT_hi{k}", [P, BLK], F32R) for k in (1, 2, 4)}
        xT_lo = {k: sb(f"xT_lo{k}", [P, BLK], F32R) for k in (1, 2, 4)}
        spare_xT = [sb("xT_hi_spare", [P, BLK], F32R), sb("xT_lo_spare", [P, BLK], F32R)]

        def spare(k, b):
            return k == 1 and is_block(b, 1) or k == 4 and is_block(b, NBLK - 1)

        def hi_of(k, b):
            return spare_xT[0][:, :] if spare(k, b) else xT_hi[k][:, :]

        def lo_of(k, b):
            return spare_xT[1][:, :] if spare(k, b) else xT_lo[k][:, :]

        x_ln = sb("x_ln", [P, TT, P])
        x_res = sb("x_res", [P, TT, P])
        x1 = sb("x1", [P, TT, P])
        x1_b = sb("x1_b", [P, TT, P])
        x2 = sb("x2", [P, TT, P])
        x2_kept = sb("x2_kept", [P, TT, P])
        x3 = sb("x3", [P, TT, P])
        ffn_sb = {k: sb(f"ffn_sb{k}", [P, BLK]) for k in (1, 4)}
        ffn_half = sb("ffn_half", [P, TT, P])
        gate_t = sb("gate_t", [P, BLK])
        val_pad = sb("val_pad", [P, SB, SEQ + 2 * PADK])
        conv = [sb("conv0", [P, SB, SEQ]), sb("conv1", [P, SB, SEQ])]
        gated = sb("gated", [P, BLK])
        y = sb("y", [P, BLK])
        y_hi = sb("y_hi", [P, BLK], F32R)
        y_lo = sb("y_lo", [P, BLK], F32R)
        res = sb("res", [P, TT, P])
        scaled = sb("scaled", [P, TT, P])
        tiny = sb("tiny", [P, TT, E])
        logit = sb("logit", [P, TT, E])
        logit_silu = sb("logit_silu", [P, TT, E])
        logit_inv = sb("logit_inv", [P, TT, E])
        score = sb("score", [P, TT, E])
        biased = sb("biased", [P, TT, E])
        hi4 = sb("hi4", [P, TT * NG, 4])
        lo4 = sb("lo4", [P, TT * NG, 4])
        hi2 = sb("hi2", [P, TT * NG, 2])
        lo2a = sb("lo2a", [P, TT * NG, 2])
        lo2b = sb("lo2b", [P, TT * NG, 2])
        lo2 = sb("lo2", [P, TT * NG, 2])
        hi1 = sb("hi1", [P, TT * NG, 1])
        lo1a = sb("lo1a", [P, TT * NG, 1])
        lo1b = sb("lo1b", [P, TT * NG, 1])
        lo1 = sb("lo1", [P, TT * NG, 1])
        gsum = sb("gsum", [P, TT, NG])
        gdiff = sb("gdiff", [P, TT, NG * NG])
        beats = sb("beats", [P, TT * NG, NG])
        grank = sb("grank", [P, TT * NG])
        gmask = sb("gmask", [P, TT * NG])
        masked0 = sb("masked0", [P, TT, E])
        masked = sb("masked", [P, TT, E + TOP])
        top8 = sb("top8", [P, TT, 8])
        replaced = sb("replaced", [P, TT, E + TOP])
        chosen = sb("chosen", [P, TT, E])
        wsum = sb("wsum", [P, TT])
        wsum_e = sb("wsum_e", [P, TT])
        winv = sb("winv", [P, TT])
        weight = sb("weight", [P, TT, E])
        w_tok = sb("w_tok", [P, TT, P], F32R)
        wT = {k: sb(f"wT{k}", [P, BLK], F32R) for k in (1, 4)}

        raw_loaded = [sem(f"raw_loaded{n}") for n in range(NBATCH)]
        vec_loaded = sem("vec_loaded")
        pool_const = sem("pool_const")
        dve_const = sem("dve_const")
        a_done = sem("a_done")
        w_transposed = sem("w_transposed")
        w_hi_done = sem("w_hi_done")
        w_lo_done = sem("w_lo_done")
        wb_ready = sem("wb_ready")
        gate_ready = sem("gate_ready")
        up_ready = sem("up_ready")
        silu_done = sem("silu_done")
        weighted_done = sem("weighted_done")
        hid_done = sem("hid_done")
        hid_hi_done = sem("hid_hi_done")
        hid_lo_done = sem("hid_lo_done")
        down_done = sem("down_done")
        ffn_copied = {k: sem(f"ffn_copied{k}") for k in (1, 4)}
        ffn_transposed = {k: sem(f"ffn_transposed{k}") for k in (1, 4)}
        ffn_added = {k: sem(f"ffn_added{k}") for k in (1, 4)}
        ln_stats = {k: sem(f"ln_stats{k}") for k in LN}
        ln_scale = {k: sem(f"ln_scale{k}") for k in LN}
        ln_normed = {k: sem(f"ln_normed{k}") for k in LN}
        xn_transposed = {k: sem(f"xn_transposed{k}") for k in (1, 2, 4)}
        xT_hi_done = {k: sem(f"xT_hi_done{k}") for k in (1, 2, 4)}
        xT_lo_done = {k: sem(f"xT_lo_done{k}") for k in (1, 2, 4)}
        logits_ready = {k: sem(f"logits_ready{k}") for k in (1, 4)}
        logit_silu_done = {k: sem(f"logit_silu_done{k}") for k in (1, 4)}
        route = {k: sem(f"route{k}") for k in (1, 4)}
        route_transposed = {k: sem(f"route_transposed{k}") for k in (1, 4)}
        wT_done = {k: sem(f"wT_done{k}") for k in (1, 4)}
        x_ln_loaded = sem("x_ln_loaded")
        x_res_loaded = sem("x_res_loaded")
        mix_gate_ready = sem("mix_gate_ready")
        mix_gate_done = sem("mix_gate_done")
        mix_val_ready = sem("mix_val_ready")
        mix_val_done = sem("mix_val_done")
        mix = sem("mix")
        first_tap_done = sem("first_tap_done")
        halved_done = sem("halved_done")
        y_hi_done = sem("y_hi_done")
        y_lo_done = sem("y_lo_done")
        mix_out_ready = sem("mix_out_ready")
        res_done = sem("res_done")
        x1_b_done = sem("x1_b_done")
        scaled_done = sem("scaled_done")
        x2_done = sem("x2_done")
        x2_kept_done = sem("x2_kept_done")
        x3_free = sem("x3_free")

        PREPARE = {"transpose 1": 1, "xT high 1": 1, "xT low 1": 1.5, "router 1": 2, "logits 1": 2.5,
                   "silu logits 1": 3, "route 1": (4.5, 5, 5.5, 6, 6.5, 8.5, 9, 9.5, 13.5, 14, 14.5)}
        CHAIN = {"copy ffn 1": 2, "transpose ffn 1": 3, "add ffn 1": 3.5, "stats 2": 4, "meanvar 2": 4,
                 "norm 2": 4, "normalise 2": 5, "add ln_b": 9, "transpose 2": 7, "xT high 2": 7,
                 "xT low 2": 7.5, "mixer gate": 9, "tanh gate": 9, "mixer value": 10, "copy value": 10,
                 "conv": (10.5, 11, 11.5, 12, 12.5, 13), "y high": 13, "y low": 13,
                 "mixer out": 15, "mixer sum": 15.5, "stats 3": 16.5}
        TAIL = {"meanvar 3": 0, "norm 3": 0, "normalise 3": 1.5, "scale 3": 2, "x2": 3, "stats 4": 3.5,
                "meanvar 4": 4, "norm 4": 4, "normalise 4": 5, "keep x2": 9, "transpose 4": 7,
                "xT high 4": 7, "xT low 4": 7.5, "router 4": 9, "logits 4": 9.5, "silu logits 4": 10,
                "route 4": (10.5, 11, 11.5, 12, 12.5, 13, 13.5, 14, 14.5, 15, 15.5)}
        OUTPUT = {"copy ffn 4": 2, "transpose ffn 4": 3, "halve ffn": 3, "add ffn 4": 6}
        NEXT = {"stats 1": 8, "meanvar 1": 8.5, "norm 1": 10, "normalise 1": 12}
        BOTH = {"copy ffn 1": 1, "transpose ffn 1": 2, "add ffn 1": 2, "stats 2": 2, "meanvar 2": 2, "norm 2": 2,
                "normalise 2": 3, "transpose 2": 4, "xT high 2": 4, "xT low 2": 4, "add ln_b": 6,
                "mixer gate": 5, "tanh gate": 5, "mixer value": 6, "copy value": 6,
                "conv": (6.5, 6.5, 7, 7, 7.5, 8), "y high": 8, "y low": 8, "mixer out": 9, "mixer sum": 9.5,
                "stats 3": 9.5, "meanvar 3": 9.5, "norm 3": 9, "normalise 3": 10, "scale 3": 9, "x2": 10.5,
                "stats 4": 10.5, "meanvar 4": 10.5, "norm 4": 10, "normalise 4": 12,
                "transpose 4": 13, "xT high 4": 13, "xT low 4": 13, "router 4": 13,
                "logits 4": 13, "silu logits 4": 13,
                "route 4": (13.5, 13.5, 14, 14.5, 15, 15.5, 15.5, 16.5, 16.5, 16.5, 16.5)}
        FIRST = {"norm 1": 0, "normalise 1": 0, "transpose 1": 3, "xT high 1": 3, "xT low 1": 3.5, "router 1": 5,
                 "logits 1": 5.5, "silu logits 1": 6,
                 "route 1": (6.5, 7, 8, 8.5, 9, 9.5, 10, 10.5, 11, 12, 13)}
        BOTH_SLOTS = NT + LAG
        AFTER_BOTH = {"stats 1": 5, "meanvar 1": 5.5, "norm 1": 7, "normalise 1": 7}
        PARTS = 11

        ROUTE = 32
        LOGITS_READ = 2
        MIX = K + 1

        block = ctx.enter_context(nc.Block())

        setup_banks = [gate_ps[0], gate_ps[1], up_ps[0], up_ps[1]]

        def setup_bank(n):
            return setup_banks[n % len(setup_banks)][:, :]


        def ffns_before(k, b):
            if k == 1:
                return 0 if is_block(b, 0) else b * 2 - 1
            return b * 2 + (1 if is_block(b, NBLK - 1) else 2)

        def first_tile(k, b):
            return ffns_before(k, b) * NT

        def first_pair(k, b):
            return ffns_before(k, b) * NPAIR

        def start_parity(k, b):
            if k == 1:
                return 0 if is_block(b, 0) else NT % 2
            return NT % 2 if is_block(b, NBLK - 1) else 0

        def ring_before(j):
            return RING if j >= RING else j + NT - max(m for m in range(NT) if m % RING == j)

        @block.sync
        def _(sp):
            def load_x_ln(b):
                if not is_block(b, 0):
                    sp.wait_ge(ln_normed[1], b)
                sp.dma_start(x_ln[:, :, :], x_blk[b]).then_inc(x_ln_loaded, 16)

            def load_x_res(b):
                if not is_block(b, 0):
                    sp.wait_ge(ffn_added[1], b)
                sp.dma_start(x_res[:, :, :], x_blk[b]).then_inc(x_res_loaded, 16)

            def store(b):
                sp.wait_ge(ffn_added[4], b + 1)
                sp.dma_start(out_blk[b], x3[:, :, :]).then_inc(x3_free, 16)

            load_x_ln(0)
            sp.dma_start(raw[:, WIN_G:WOUT, :], W_in.rearrange("(n p) h -> p n h", p=P))\
              .then_inc(raw_loaded[0], 16)
            sp.dma_start(raw[:, WOUT, :], W_out).then_inc(raw_loaded[0], 16)
            sp.wait_ge(dve_const, 1)
            sp.dma_start(raw[0:E, WROUTER, :], router_w).then_inc(raw_loaded[0], 16)
            gate_v = gate_w.rearrange("e i h -> (e i) h").rearrange("(n p) h -> p n h", p=P)
            up_v = up_w.rearrange("e i h -> (e i) h").rearrange("(n p) h -> p n h", p=P)
            down_v = down_w.rearrange("e h i -> h e i")
            for q in range(4):
                for n, (tile, view) in enumerate(((gate_tile, gate_v), (up_tile, up_v))):
                    sp.dma_start(raw[:, tile(4 * q):tile(4 * q) + 4, :], view[:, 4 * q:4 * q + 4, :])\
                      .then_inc(raw_loaded[1 + 3 * q + n], 16)
                dst = raw[:, down_tile(4 * q):down_tile(4 * q) + 4, :]
                sp.dma_start(dst.rearrange("p n (e i) -> p (n e) i", e=2), down_v[:, 8 * q:8 * q + 8, :])\
                  .then_inc(raw_loaded[3 + 3 * q], 16)
                if q == 0:
                    sp.dma_start(bias_b[:, :], router_b.partition_broadcast(P)).then_inc(vec_loaded, 16)
                    sp.dma_start(lnw_b[:, :], ln_w.partition_broadcast(P)).then_inc(vec_loaded, 16)
                    sp.dma_start(lnb_b[:, :], ln_b.partition_broadcast(P)).then_inc(vec_loaded, 16)
                    sp.dma_start(taps[:, :], conv_w.rearrange("d o k -> d (o k)")).then_inc(vec_loaded, 16)
                    sp.dma_start(cbias[:, :], conv_b.unsqueeze(1)).then_inc(vec_loaded, 16)
                    sp.dma_start(a_raw[:, :], a_param.unsqueeze(1)).then_inc(vec_loaded, 16)
            for n, w in enumerate((sh_gate, sh_up, sh_down)):
                sp.dma_start(raw[:, 52 + n, :], w).then_inc(raw_loaded[NBATCH - 1], 16)
            load_x_res(0)

            load_x_ln(2)
            load_x_res(1)
            with sp.Fori(2, NBLK - 1) as i:
                load_x_res(i)
                load_x_ln(i + 1)
                store(i - 2)
            load_x_res(NBLK - 1)
            for b in range(NBLK - 3, NBLK):
                store(b)
            sp.wait_ge(x3_free, 16 + 16 * NBLK)

        @block.gpsimd
        def _(pool):
            def hidden_low(k, b, j):
                n = first_tile(k, b) + j
                s = j % RING
                pool.wait_ge(hid_hi_done, n + 1)
                nc.gpsimd.tensor_tensor(hid_lo[s][:, :], hid[s][:, :], hid_hi[s][:, :].bitcast(F32),
                                        ALU.subtract).then_inc(hid_lo_done, 1)

            def norm_scale(k, b):
                st = Steps(pool, ln_scale[k], b * 4)
                pool.wait_ge(ln_stats[k], b * 2 + 2)
                st.done(nc.gpsimd.tensor_tensor(neg_mean[k][:, :], zeros[:, 0:TT], meanvar[k][:, :, 0],
                                                ALU.subtract))
                st.done(nc.gpsimd.tensor_tensor(var_eps[k][:, :], meanvar[k][:, :, 1], eps[:, :], ALU.add))
                st.wait()
                st.done(nc.gpsimd.tensor_tensor(rstd[k][:, :], var_eps[k][:, :], neg_half[:, :], ALU.pow))
                st.wait()
                st.done(nc.gpsimd.tensor_tensor(shift[k][:, :], neg_mean[k][:, :], rstd[k][:, :], ALU.mult))

            def output_add(b):
                pool.wait_ge(halved_done, b + 1)
                pool.wait_ge(x3_free, 16 + b * 16)
                nc.gpsimd.tensor_tensor(x3[:, :, :], ffn_half[:, :, :], x2_kept[:, :, :], ALU.add)\
                  .then_inc(ffn_added[4], 1)

            def unit(main, steps, chain=None, tail=None, prepare=None, output=None, slots=NT, **_):
                for j in range(slots):
                    if j == steps.get("norm 3"):
                        norm_scale(3, tail)
                    if j == steps.get("scale 3"):
                        pool.wait_ge(ln_normed[3], tail + 1)
                        nc.gpsimd.tensor_tensor(scaled[:, :, :], normed[3][:, :, :],
                                                lnw_b[:, :].unsqueeze(1).broadcast_to([P, TT, P]), ALU.mult)\
                          .then_inc(scaled_done, 1)
                    if j == steps.get("add ffn 4"):
                        output_add(output)
                    if j == steps.get("norm 4"):
                        norm_scale(4, tail)
                    if j == steps.get("norm 2"):
                        norm_scale(2, chain)
                    if j == steps.get("add ln_b"):
                        bc = lnb_b[:, :].unsqueeze(1).broadcast_to([P, TT, P])
                        nc.gpsimd.tensor_tensor(x1_b[:, :, :], x1[:, :, :], bc, ALU.add).then_inc(x1_b_done, 1)
                    if j == steps.get("y low"):
                        pool.wait_ge(y_hi_done, chain + 1)
                        nc.gpsimd.tensor_tensor(y_lo[:, :], y[:, :], y_hi[:, :].bitcast(F32),
                                                ALU.subtract).then_inc(y_lo_done, 1)
                    if j == steps.get("norm 1"):
                        norm_scale(1, prepare)
                    if j < NT:
                        hidden_low(*main, j)

            const = Steps(pool, pool_const, 0)
            nc.gpsimd.memset(x3[:, 0, 0:1], 0.0).then_inc(x3_free, 16)
            const.done(nc.gpsimd.memset(zeros[:, :], 0.0))
            const.done(nc.gpsimd.memset(neg_half[:, :], -0.5))
            const.done(nc.gpsimd.memset(eps[:, :], EPS))
            const.wait()
            const.done(nc.gpsimd.affine_select(out=ident[:, :], in_=zeros[:, :], fill=1.0,
                                               compare_op=ALU.not_equal, base=0,
                                               pattern=[[-1, P]], channel_multiplier=1))
            assert const.n == 4
            norm_scale(1, 0)
            const.done(nc.gpsimd.affine_select(
                out=beat_at[:, :, :], in_=zeros[:, 0:NG * NG].rearrange("p (g h) -> p g h", g=NG),
                fill=1e-37, compare_op=ALU.is_gt, base=0, pattern=[[1, NG], [-1, NG]], channel_multiplier=0))
            spread = [[-2, NPAIR], [-1, 2], [0, I]]
            as_rows = lambda t: t[:, :, :].rearrange("p n (e i) -> p n e i", e=2)
            const.done(nc.gpsimd.affine_select(out=as_rows(pick),
                                               in_=zeros[:, :].rearrange("p (e i) -> p e i", e=2).unsqueeze(1)
                                               .broadcast_to([P, NPAIR, 2, I]), fill=1.0,
                                               compare_op=ALU.not_equal, base=0,
                                               pattern=spread, channel_multiplier=1))
            const.wait()
            const.done(nc.gpsimd.affine_select(out=as_rows(pick), in_=as_rows(pick).bitcast(F32), fill=1.0,
                                               compare_op=ALU.not_equal, base=-E,
                                               pattern=spread, channel_multiplier=1))
            assert const.n == 7
            pool.wait_ge(vec_loaded, 16 * 6)
            unit((1, 0), FIRST, prepare=1)
            unit((1, 1), {**BOTH, **AFTER_BOTH}, before=(1, 0), chain=0, tail=0, prepare=2, slots=BOTH_SLOTS)
            unit((4, 0), {**CHAIN, **PREPARE}, chain=1, prepare=2)
            with pool.Fori(2, NBLK - 1) as i:
                unit((1, i), {**TAIL, **OUTPUT, **NEXT}, before=(4, i - 2), output=i - 2, tail=i - 1, prepare=i + 1)
                unit((4, i - 1), {**CHAIN, **PREPARE}, before=(1, i), chain=i, prepare=i + 1)
            unit((1, NBLK - 1), {**TAIL, **OUTPUT}, before=(4, NBLK - 3), output=NBLK - 3, tail=NBLK - 2)
            unit((4, NBLK - 2), BOTH, before=(1, NBLK - 1), chain=NBLK - 1, tail=NBLK - 1,
                 slots=BOTH_SLOTS)
            unit((4, NBLK - 1), {**OUTPUT, "keep x2": 9}, output=NBLK - 2, tail=NBLK - 1)
            output_add(NBLK - 1)

        @block.scalar
        def _(act):
            def weight_high(n):
                act.wait_ge(w_transposed, n + 1)
                nc.scalar.activation(wt_hi[:, 4 * n:4 * n + 4, :].rearrange("p n c -> p (n c)"),
                                     setup_bank(n), ACT.Copy).then_inc(w_hi_done, 1)

            def silu_tile(k, b, j):
                n = first_tile(k, b) + j
                s = (start_parity(k, b) + j) % 2
                act.wait_ge(gate_ready, n + 1)
                if not (isinstance(n, int) and n < 2):
                    act.wait_ge(hid_done, n - 1)
                nc.scalar.activation(silu_sb[s][:, :], gate_ps[s][:, :], ACT.Silu).then_inc(silu_done, 1)

            def hidden_high(k, b, j):
                n = first_tile(k, b) + j
                s = j % RING
                act.wait_ge(hid_done, n + 1)
                last = n - ring_before(j)
                if not (isinstance(last, int) and last < 0):
                    act.wait_ge(down_done, last + 1)
                nc.scalar.activation(hid_hi[s][:, :], hid[s][:, :], ACT.Copy).then_inc(hid_hi_done, 1)

            def ffn_copy(k, b):
                act.wait_ge(down_done, first_tile(k, b) + NT)
                nc.scalar.activation(ffn_sb[k][:, :], down_ps[:, :], ACT.Copy).then_inc(ffn_copied[k], 1)

            def halve_ffn(b):
                act.wait_ge(ffn_transposed[4], b + 1)
                nc.scalar.activation(ffn_half[:, :, :], side_td, ACT.Copy, scale=0.5).then_inc(halved_done, 1)

            def xT_high(k, b):
                act.wait_ge(xn_transposed[k], b + 1)
                nc.scalar.activation(hi_of(k, b), side[:, :], ACT.Copy).then_inc(xT_hi_done[k], 1)

            def silu_logits(k, b):
                act.wait_ge(route[k], b * ROUTE + 2)
                nc.scalar.activation(logit_silu[:, :, :], logit[:, :, :], ACT.Silu)\
                  .then_inc(logit_silu_done[k], 1)

            def wT_copy(k, b):
                act.wait_ge(route_transposed[k], b + 1)
                nc.scalar.activation(wT[k][:, :], side[:, :], ACT.Copy).then_inc(wT_done[k], 1)

            def normalise(k, b, src):
                act.wait_ge(ln_scale[k], b * 4 + 4)
                for t in range(TT):
                    last = nc.scalar.activation(normed[k][:, t, :], src[:, t, :], ACT.Identity,
                                                bias=shift[k][:, t:t + 1], scale=rstd[k][:, t:t + 1])
                last.then_inc(ln_normed[k], 1)

            def unit(main, steps, before=None, chain=None, tail=None, prepare=None,
                     output=None, slots=NT):
                for j in range(slots):
                    if j < NT:
                        silu_tile(*main, j)
                    if j == 0:
                        wT_copy(*main)
                    if j == 0 and before is not None:
                        hidden_high(*before, NT - 1)
                    if 0 < j <= NT:
                        hidden_high(*main, j - 1)
                    if j == steps.get("copy ffn 4"):
                        ffn_copy(4, output)
                    if j == steps.get("halve ffn"):
                        halve_ffn(output)
                    if j == steps.get("normalise 1"):
                        normalise(1, prepare, x_ln)
                    if j == steps.get("xT high 1"):
                        xT_high(1, prepare)
                    if j == steps.get("copy ffn 1"):
                        ffn_copy(1, chain)
                    if j == steps.get("silu logits 1"):
                        silu_logits(1, prepare)
                    if j == steps.get("normalise 2"):
                        normalise(2, chain, x1)
                    if j == steps.get("xT high 2"):
                        xT_high(2, chain)
                    if j == steps.get("tanh gate"):
                        act.wait_ge(mix_gate_ready, chain + 1)
                        nc.scalar.activation(gate_t[:, :], side[:, :], ACT.Tanh, scale=0.5)\
                          .then_inc(mix_gate_done, 1)
                    if j == steps.get("copy value"):
                        act.wait_ge(mix_val_ready, chain + 1)
                        nc.scalar.activation(val_pad[:, :, PADK:PADK + SEQ],
                                             side[:, :].rearrange("p (s t) -> p s t", s=SB), ACT.Copy)\
                          .then_inc(mix_val_done, 1)
                        act.wait_ge(mix_val_done, chain + 1)
                        if not is_block(chain, 0):
                            act.wait_ge(mix, chain * MIX)
                        nc.scalar.activation(conv[0][:, :, :], val_pad[:, :, 0:SEQ], ACT.Identity,
                                             bias=cbias_half[:, 0:1], scale=taps_half[:, 0:1])\
                          .then_inc(first_tap_done, 1)
                    if j == steps.get("y high"):
                        act.wait_ge(mix, chain * MIX + MIX)
                        nc.scalar.activation(y_hi[:, :], y[:, :], ACT.Copy).then_inc(y_hi_done, 1)
                    if j == steps.get("normalise 4"):
                        normalise(4, tail, x2)
                    if j == steps.get("keep x2"):
                        if not is_block(tail, 0):
                            act.wait_ge(ffn_added[4], tail)
                        nc.scalar.activation(x2_kept[:, :, :], x2[:, :, :], ACT.Copy).then_inc(x2_kept_done, 1)
                    if j == steps.get("xT high 4"):
                        xT_high(4, tail)
                    if j == steps.get("silu logits 4"):
                        silu_logits(4, tail)

            act.wait_ge(pool_const, 1)
            nc.scalar.activation(silu_sb[0][:, 0:1], zeros[:, 0:1], ACT.Silu)
            for n in range(NBATCH):
                weight_high(n)
                if n == 0:
                    normalise(1, 0, x_ln)
                if n == 1:
                    xT_high(1, 0)
                    act.wait_ge(ln_normed[1], 1)
                    act.dma_start(x_ln[:, :, :], x_blk[1]).then_inc(x_ln_loaded, 16)
                if n == 3:
                    silu_logits(1, 0)
                if n == 6:
                    act.wait_ge(vec_loaded, 16 * 6)
                    nc.scalar.activation(a_tanh[:, :], a_raw[:, :], ACT.Tanh).then_inc(a_done, 1)
            unit((1, 0), FIRST, prepare=1)
            unit((1, 1), {**BOTH, **AFTER_BOTH, "keep x2": 15}, before=(1, 0), chain=0, tail=0, prepare=2,
                 slots=BOTH_SLOTS)
            unit((4, 0), {**CHAIN, **PREPARE}, chain=1, prepare=2)
            with act.Fori(2, NBLK - 1) as i:
                unit((1, i), {**TAIL, **OUTPUT, **NEXT}, before=(4, i - 2), output=i - 2, tail=i - 1, prepare=i + 1)
                unit((4, i - 1), {**CHAIN, **PREPARE}, before=(1, i), chain=i, prepare=i + 1)
            unit((1, NBLK - 1), {**TAIL, **OUTPUT}, before=(4, NBLK - 3), output=NBLK - 3, tail=NBLK - 2)
            unit((4, NBLK - 2), BOTH, before=(1, NBLK - 1), chain=NBLK - 1, tail=NBLK - 1,
                 slots=BOTH_SLOTS)
            unit((4, NBLK - 1), {**OUTPUT, "keep x2": 9}, output=NBLK - 2, tail=NBLK - 1,
                 slots=NT + 1)
            ffn_copy(4, NBLK - 1)
            halve_ffn(NBLK - 1)

        @block.vector
        def _(dve):
            V = nc.vector

            def weight_low(n):
                dve.wait_ge(w_hi_done, n + 1)
                V.tensor_tensor(wt_lo[:, 4 * n:4 * n + 4, :].rearrange("p n c -> p (n c)"), setup_bank(n),
                                wt_hi[:, 4 * n:4 * n + 4, :].rearrange("p n c -> p (n c)").bitcast(F32),
                                ALU.subtract).then_inc(w_lo_done, 1)

            def weigh_tile(k, b, j):
                n = first_tile(k, b) + j
                s = (start_parity(k, b) + j) % 2
                dve.wait_ge(silu_done, n + 1)
                dve.wait_ge(wb_ready, first_pair(k, b) + j + 1)
                V.tensor_tensor(weighted[s][:, :], silu_sb[s][:, :], wb_ps[j % 2][:, :], ALU.mult)\
                 .then_inc(weighted_done, 1)

            def hidden_tile(k, b, j):
                n = first_tile(k, b) + j
                s = (start_parity(k, b) + j) % 2
                dve.wait_ge(up_ready, n + 1)
                if j < NPAIR:
                    dve.wait_ge(weighted_done, first_pair(k, b) + j + 1)
                else:
                    dve.wait_ge(silu_done, n + 1)
                last = n - ring_before(j)
                if not (isinstance(last, int) and last < 0):
                    dve.wait_ge(hid_lo_done, last + 1)
                factor = weighted[s] if j < NPAIR else silu_sb[s]
                V.tensor_tensor(hid[j % RING][:, :], factor[:, :], up_ps[s][:, :], ALU.mult).then_inc(hid_done, 1)

            def norm_stats(k, src):
                for t in range(TT):
                    last = V.bn_stats(stats[k][:, t, :], src[:, t, :])
                last.then_inc(ln_stats[k], 1)

            def norm_meanvar(k, b):
                dve.wait_ge(ln_stats[k], b * 2 + 1)
                V.memset(hold[:, :], 0.0)
                for t in range(TT):
                    last = V.bn_aggr(meanvar[k][:, t, :], stats[k][:, t, :])
                last.then_inc(ln_stats[k], 1)

            def xT_low(k, b):
                dve.wait_ge(xT_hi_done[k], b + 1)
                V.tensor_tensor(lo_of(k, b), side[:, :], hi_of(k, b).bitcast(F32), ALU.subtract)\
                 .then_inc(xT_lo_done[k], 1)

            def route_logits(k, b, st):
                dve.wait_ge(logits_ready[k], b + 1)
                st.done(V.tensor_scalar(tiny[:, :, :], side_te, -1e-9, 1e-8, ALU.is_ge, ALU.mult))
                st.wait()
                st.done(V.tensor_tensor(logit[:, :, :], tiny[:, :, :], side_te, ALU.add))
                st.wait()
                st.done(V.reciprocal(logit_inv[:, :, :], logit[:, :, :]))
                st.wait()

            def route_part(k, b, st, part):
                if part == 0:
                    dve.wait_ge(logit_silu_done[k], b + 1)
                    st.wait()
                    st.done(V.tensor_tensor(score[:, :, :], logit_silu[:, :, :], logit_inv[:, :, :], ALU.mult))
                    st.wait()
                    st.done(V.tensor_tensor(biased[:, :, :], score[:, :, :],
                                            bias_b[:, :].unsqueeze(1).broadcast_to([P, TT, E]), ALU.add))
                if part == 1:
                    st.wait()
                    g8 = biased[:, :, :].rearrange("p t (g c) -> p (t g) c", g=NG)
                    st.done(V.tensor_tensor(hi4[:, :, :], g8[:, :, 0:4], g8[:, :, 4:8], ALU.max))
                    st.done(V.tensor_tensor(lo4[:, :, :], g8[:, :, 0:4], g8[:, :, 4:8], ALU.min))
                    st.wait()
                    st.done(V.tensor_tensor(hi2[:, :, :], hi4[:, :, 0:2], hi4[:, :, 2:4], ALU.max))
                    st.done(V.tensor_tensor(lo2a[:, :, :], hi4[:, :, 0:2], hi4[:, :, 2:4], ALU.min))
                    st.done(V.tensor_tensor(lo2b[:, :, :], lo4[:, :, 0:2], lo4[:, :, 2:4], ALU.max))
                if part == 2:
                    st.wait()
                    st.done(V.tensor_tensor(lo2[:, :, :], lo2a[:, :, :], lo2b[:, :, :], ALU.max))
                    st.done(V.tensor_tensor(hi1[:, :, :], hi2[:, :, 0:1], hi2[:, :, 1:2], ALU.max))
                    st.done(V.tensor_tensor(lo1a[:, :, :], hi2[:, :, 0:1], hi2[:, :, 1:2], ALU.min))
                    st.wait()
                    st.done(V.tensor_tensor(lo1b[:, :, :], lo2[:, :, 0:1], lo2[:, :, 1:2], ALU.max))
                if part == 3:
                    st.wait()
                    st.done(V.tensor_tensor(lo1[:, :, :], lo1a[:, :, :], lo1b[:, :, :], ALU.max))
                    st.wait()
                    st.done(V.tensor_tensor(gsum[:, :, :].rearrange("p t g -> p (t g)").unsqueeze(2),
                                            hi1[:, :, :], lo1[:, :, :], ALU.add))
                if part == 4:
                    st.wait()
                    for t in range(TT):
                        last = V.tensor_tensor(gdiff[:, t, :].rearrange("p (g h) -> p g h", g=NG),
                                               gsum[:, t, :].unsqueeze(1).broadcast_to([P, NG, NG]),
                                               gsum[:, t, :].unsqueeze(2).broadcast_to([P, NG, NG]), ALU.subtract)
                    st.done(last)
                    st.wait()
                    st.done(V.tensor_tensor(beats[:, :, :].rearrange("p (t g) h -> p t (g h)", t=TT), gdiff[:, :, :],
                                            beat_at[:, :, :].rearrange("p g h -> p (g h)").unsqueeze(1)
                                            .broadcast_to([P, TT, NG * NG]), ALU.is_ge))
                if part == 5:
                    st.wait()
                    st.done(V.tensor_reduce(grank[:, :], beats[:, :, :], AX.X, ALU.add))
                    st.wait()
                    st.done(V.tensor_scalar(gmask[:, :], grank[:, :], float(GTOP), None, ALU.is_lt))
                if part == 6:
                    st.wait()
                    st.done(V.tensor_tensor(masked0[:, :, :].rearrange("p t (g c) -> p (t g) c", g=NG),
                                            biased[:, :, :].rearrange("p t (g c) -> p (t g) c", g=NG),
                                            gmask[:, :].unsqueeze(2).broadcast_to([P, TT * NG, PG]), ALU.mult))
                    st.wait()
                    st.done(V.tensor_scalar(masked[:, :, 0:E], masked0[:, :, :], 0.0, None, ALU.add))
                if part == 7:
                    st.wait()
                    V.memset(hold[:, :], 0.0)
                    for t in range(TT):
                        last = V.max(top8[:, t, :], masked[:, t, 0:E])
                    st.done(last)
                if part == 8:
                    st.wait()
                    st.done(V.memset(top8[:, :, TOP:8], FAR))
                    st.wait()
                    V.memset(hold[:, :], 0.0)
                    for t in range(TT):
                        last = V.match_replace(replaced[:, t, :], top8[:, t, :], masked[:, t, :], GONE)
                    st.done(last)
                if part == 9:
                    st.wait()
                    st.done(V.scalar_tensor_tensor(chosen[:, :, :], replaced[:, :, 0:E], (FAR + GONE) / 2,
                                                   score[:, :, :], ALU.is_lt, ALU.mult))
                    st.wait()
                    st.done(V.tensor_reduce(wsum[:, :], chosen[:, :, :], AX.X, ALU.add))
                    st.wait()
                    st.done(V.tensor_scalar(wsum_e[:, :], wsum[:, :], 1e-20, None, ALU.add))
                if part == 10:
                    st.wait()
                    st.done(V.reciprocal(winv[:, :], wsum_e[:, :]))
                    st.wait()
                    st.done(V.scalar_tensor_tensor(weight[:, :, :], chosen[:, :, :], SCALE,
                                                   winv[:, :].unsqueeze(2).broadcast_to([P, TT, E]),
                                                   ALU.mult, ALU.mult))
                    st.wait()
                    st.done(V.tensor_copy(w_tok[:, :, 0:E], weight[:, :, :]))
                    st.wait()
                    st.done(V.tensor_tensor(w_tok[:, :, E:2 * E], weight[:, :, :], w_tok[:, :, 0:E].bitcast(F32),
                                            ALU.subtract))
                    assert st.n == ROUTE

            def conv_tap(i, st, t):
                src = val_pad[:, :, t:t + SEQ]
                if t == 1:
                    dve.wait_ge(first_tap_done, i + 1)
                else:
                    st.wait()
                st.done(V.scalar_tensor_tensor(conv[t % 2][:, :, :], src, taps_half[:, t:t + 1],
                                               conv[(t + 1) % 2][:, :, :], ALU.mult, ALU.add))

            def gate_value(i, st):
                dve.wait_ge(mix_gate_done, i + 1)
                st.wait()
                st.done(V.scalar_tensor_tensor(gated[:, :].rearrange("p (s t) -> p s t", s=SB),
                                               gate_t[:, :].rearrange("p (s t) -> p s t", s=SB), 1.0,
                                               conv[(K - 1) % 2][:, :, :], ALU.add, ALU.mult))

            def recur(i, st):
                st.wait()
                if not is_block(i, 0):
                    dve.wait_ge(y_lo_done, i)
                st.done(V.tensor_tensor_scan(y[:, :], decay[:, :], gated[:, :], 0.0, ALU.mult, ALU.add))
                assert st.n == MIX

            def beside(at, steps, st1, st4, mx, chain, tail, prepare, output):
                if at == steps.get("xT low 2"):
                    xT_low(2, chain)
                if at == steps.get("mixer sum"):
                    dve.wait_ge(mix_out_ready, chain + 1)
                    V.tensor_tensor(res[:, :, :], side_td, normed[2][:, :, :], ALU.add).then_inc(res_done, 1)
                if at == steps.get("stats 3"):
                    dve.wait_ge(res_done, chain + 1)
                    norm_stats(3, res)
                if at == steps.get("normalise 3"):
                    dve.wait_ge(ln_scale[3], tail * 4 + 4)
                    for t in range(TT):
                        last = V.tensor_scalar(normed[3][:, t, :], res[:, t, :], rstd[3][:, t:t + 1],
                                               shift[3][:, t:t + 1], ALU.mult, ALU.add)
                    last.then_inc(ln_normed[3], 1)
                if at == steps.get("x2"):
                    dve.wait_ge(x1_b_done, tail + 1)
                    dve.wait_ge(scaled_done, tail + 1)
                    if not is_block(tail, 0):
                        dve.wait_ge(x2_kept_done, tail)
                    V.tensor_tensor(x2[:, :, :], scaled[:, :, :], x1_b[:, :, :], ALU.add).then_inc(x2_done, 1)
                if at == steps.get("stats 4"):
                    dve.wait_ge(x2_done, tail + 1)
                    norm_stats(4, x2)
                if at == steps.get("xT low 4"):
                    xT_low(4, tail)
                if at == steps.get("logits 4"):
                    route_logits(4, tail, st4)
                for part in range(PARTS):
                    if "route 4" in steps and at == steps["route 4"][part]:
                        route_part(4, tail, st4, part)
                if at == steps.get("xT low 1"):
                    xT_low(1, prepare)
                if at == steps.get("logits 1"):
                    route_logits(1, prepare, st1)
                if at == steps.get("add ffn 1"):
                    dve.wait_ge(x_res_loaded, chain * 16 + 16)
                    dve.wait_ge(ffn_transposed[1], chain + 1)
                    V.scalar_tensor_tensor(x1[:, :, :], side_td, 0.5, x_res[:, :, :], ALU.mult, ALU.add)\
                     .then_inc(ffn_added[1], 1)
                if at == steps.get("stats 2"):
                    dve.wait_ge(ffn_added[1], chain + 1)
                    norm_stats(2, x1)
                for part in range(PARTS):
                    if "route 1" in steps and at == steps["route 1"][part]:
                        route_part(1, prepare, st1, part)
                if "conv" in steps:
                    for t in range(1, K):
                        if at == steps["conv"][t - 1]:
                            conv_tap(chain, mx, t)
                    if at == steps["conv"][K - 1]:
                        gate_value(chain, mx)
                    if at == steps["conv"][K]:
                        recur(chain, mx)
                if at == steps.get("stats 1"):
                    dve.wait_ge(x_ln_loaded, prepare * 16 + 16)
                    norm_stats(1, x_ln)
                for k, b in ((1, prepare), (2, chain), (3, chain if tail is None else tail), (4, tail)):
                    if at == steps.get(f"meanvar {k}"):
                        norm_meanvar(k, b)

            def unit(main, steps, chain=None, tail=None, prepare=None, output=None, slots=NT, **_):
                st1 = Steps(dve, route[1], prepare * ROUTE) if "route 1" in steps else None
                st4 = Steps(dve, route[4], tail * ROUTE) if "route 4" in steps else None
                mx = Steps(dve, mix, chain * MIX) if "conv" in steps else None
                for j in range(slots):
                    if j < NPAIR:
                        weigh_tile(*main, j)
                    beside(j, steps, st1, st4, mx, chain, tail, prepare, output)
                    if j < NT:
                        hidden_tile(*main, j)
                    beside(j + 0.5, steps, st1, st4, mx, chain, tail, prepare, output)

            const = Steps(dve, dve_const, 0)
            const.done(V.memset(raw[:, WROUTER, :], 0.0))
            const.done(V.memset(val_pad[:, :, :], 0.0))
            const.done(V.memset(masked[:, :, :], FAR))
            const.done(V.memset(ones[:, :], 1.0))
            const.done(V.memset(w_tok[:, :, :].bitcast(F32), 0.0))
            dve.wait_ge(x_ln_loaded, 16)
            norm_stats(1, x_ln)
            norm_meanvar(1, 0)
            first = Steps(dve, route[1], 0)
            for n in range(4):
                if n == 3:
                    route_logits(1, 0, first)
                weight_low(n)
                if n == 1:
                    xT_low(1, 0)
            dve.wait_ge(vec_loaded, 16 * 6)
            dve.wait_ge(pool_const, 7)
            for part in range(PARTS):
                for n in range(4 + 2 * part, min(6 + 2 * part, NBATCH)):
                    weight_low(n)
                route_part(1, 0, first, part)
            dve.wait_ge(x_ln_loaded, 32)
            norm_stats(1, x_ln)
            norm_meanvar(1, 1)
            const.done(V.tensor_scalar(taps_half[:, :], taps[:, :], 0.5, None, ALU.mult))
            const.done(V.tensor_scalar(cbias_half[:, :], cbias[:, :], 0.5, None, ALU.mult))
            dve.wait_ge(a_done, 1)
            const.wait()
            const.done(V.tensor_scalar(decay[:, :], ones[:, :], a_tanh[:, 0:1], None, ALU.mult))
            const.wait()
            const.done(V.memset(decay[:, :].rearrange("p (s t) -> p s t", s=SB)[:, :, 0:1], 0.0))
            const.wait()
            unit((1, 0), FIRST, prepare=1)
            unit((1, 1), {**BOTH, **AFTER_BOTH}, before=(1, 0), chain=0, tail=0, prepare=2, slots=BOTH_SLOTS)
            unit((4, 0), {**CHAIN, **PREPARE}, chain=1, prepare=2)
            with dve.Fori(2, NBLK - 1) as i:
                unit((1, i), {**TAIL, **OUTPUT, **NEXT}, before=(4, i - 2), output=i - 2, tail=i - 1, prepare=i + 1)
                unit((4, i - 1), {**CHAIN, **PREPARE}, before=(1, i), chain=i, prepare=i + 1)
            unit((1, NBLK - 1), {**TAIL, **OUTPUT}, before=(4, NBLK - 3), output=NBLK - 3, tail=NBLK - 2)
            unit((4, NBLK - 2), BOTH, before=(1, NBLK - 1), chain=NBLK - 1, tail=NBLK - 1,
                 slots=BOTH_SLOTS)
            unit((4, NBLK - 1), {**OUTPUT, "keep x2": 9}, output=NBLK - 2, tail=NBLK - 1)

        @block.tensor
        def _(pe):
            def product(dst, w, moving_hi, moving_lo, w_lo, start, stop):
                nc.tensor.matmul(dst, w, moving_hi, start=start, stop=False)
                nc.tensor.matmul(dst, w, moving_lo, start=False, stop=False)
                return nc.tensor.matmul(dst, w_lo, moving_hi, start=False, stop=stop)

            def weights(n):
                pe.wait_ge(raw_loaded[n], {0: 48, NBATCH - 1: 48}.get(n, 16))
                if n >= len(setup_banks):
                    pe.wait_ge(w_lo_done, n - len(setup_banks) + 1)
                for t in range(4):
                    if 4 * n + t <= down_tile(NPAIR):
                        last = nc.tensor.transpose(setup_bank(n)[:, t * P:(t + 1) * P], raw[:, 4 * n + t, :],
                                                   ident[:, :])
                    else:
                        last = nc.tensor.transpose(setup_bank(n)[:, t * P:(t + 1) * P], raw[:, WROUTER, :],
                                                   ident[:, :])
                last.then_inc(w_transposed, 1)

            def spread_weights(k, b, j):
                r = first_pair(k, b) + j
                if not (isinstance(r, int) and r < 2):
                    pe.wait_ge(weighted_done, r - 1)
                nc.tensor.matmul(wb_ps[j % 2][:, :], pick[:, j, :], wT[k][:, :], start=True, stop=True)\
                  .then_inc(wb_ready, 1)

            def up_tiles(k, b, j):
                n = first_tile(k, b) + j
                s = (start_parity(k, b) + j) % 2
                late = not (isinstance(n, int) and n < 2)
                if late:
                    pe.wait_ge(silu_done, n - 1)
                g, u = gate_tile(j), up_tile(j)
                product(gate_ps[s][:, :], wt_hi[:, g, :], hi_of(k, b), lo_of(k, b), wt_lo[:, g, :],
                        True, True).then_inc(gate_ready, 1)
                if j == 1:
                    pe.wait_ge(wT_done[k], b + 1)
                    spread_weights(k, b, 0)
                if 0 < j < NPAIR:
                    spread_weights(k, b, j)
                if late:
                    pe.wait_ge(hid_done, n - 1)
                product(up_ps[s][:, :], wt_hi[:, u, :], hi_of(k, b), lo_of(k, b), wt_lo[:, u, :],
                        True, True).then_inc(up_ready, 1)

            def down(k, b, j):
                n = first_tile(k, b) + j
                s = j % RING
                w = down_tile(j)
                if j == 0:
                    if k == 4:
                        if is_block(b, NBLK - 1):
                            pe.wait_ge(ffn_copied[4], b)
                        else:
                            pe.wait_ge(ffn_copied[1], b + 2)
                    elif not is_block(b, 0):
                        if is_block(b, 1):
                            pe.wait_ge(ffn_copied[1], 1)
                        else:
                            pe.wait_ge(ffn_copied[4], b - 1)
                pe.wait_ge(hid_hi_done, n + 1)
                nc.tensor.matmul(down_ps[:, :], wt_hi[:, w, :], hid_hi[s][:, :], start=(j == 0), stop=False)
                nc.tensor.matmul(down_ps[:, :], wt_lo[:, w, :], hid_hi[s][:, :], start=False, stop=False)
                pe.wait_ge(hid_lo_done, n + 1)
                nc.tensor.matmul(down_ps[:, :], wt_hi[:, w, :], hid_lo[s][:, :], start=False,
                                 stop=(j == NT - 1)).then_inc(down_done, 1)

            def transpose4(src, done):
                for t in range(TT):
                    last = nc.tensor.transpose(side[:, t * P:(t + 1) * P], src(t), ident[:, :])
                last.then_inc(done, 1)

            def transpose_norm(k, b):
                pe.wait_ge(ln_normed[k], b + 1)
                transpose4(lambda t: normed[k][:, t, :], xn_transposed[k])

            def transpose_ffn(k, b):
                pe.wait_ge(ffn_copied[k], b + 1)
                transpose4(lambda t: ffn_sb[k][:, t * P:(t + 1) * P], ffn_transposed[k])

            def router(k, b):
                pe.wait_ge(xT_lo_done[k], b + 1)
                w_hi, w_lo = wt_hi[:, WROUTER, 0:E], wt_lo[:, WROUTER, 0:E]
                for t in range(TT):
                    rows = slice(t * P, (t + 1) * P)
                    x_hi, x_lo = hi_of(k, b)[:, rows], lo_of(k, b)[:, rows]
                    nc.tensor.matmul(side_te[:, t, :], x_hi, w_hi, start=True, stop=False)
                    nc.tensor.matmul(side_te[:, t, :], x_hi, w_lo, start=False, stop=False)
                    last = nc.tensor.matmul(side_te[:, t, :], x_lo, w_hi, start=False, stop=True)
                last.then_inc(logits_ready[k], 1)

            def transpose_route(k, b):
                pe.wait_ge(route[k], b * ROUTE + ROUTE)
                transpose4(lambda t: w_tok[:, t, :].bitcast(F32), route_transposed[k])

            def mixer_out(b):
                for t in range(TT):
                    rows = slice(t * P, (t + 1) * P)
                    nc.tensor.matmul(side[:, rows], y_hi[:, rows], wt_hi[:, WOUT, :], start=True, stop=False)
                    nc.tensor.matmul(side[:, rows], y_hi[:, rows], wt_lo[:, WOUT, :], start=False, stop=False)
                    last = nc.tensor.matmul(side[:, rows], y_lo[:, rows], wt_hi[:, WOUT, :],
                                            start=False, stop=True)
                last.then_inc(mix_out_ready, 1)


            def unit(main, steps, free, before=None, chain=None, tail=None, prepare=None,
                     output=None, slots=NT):
                pe.wait_ge(xT_lo_done[main[0]], main[1] + 1)
                for j in range(slots):
                    if j < NT:
                        up_tiles(*main, j)
                    if j == 0:
                        if "weights" in free:
                            pe.wait_ge(*free["weights"])
                        transpose_route(*main)
                    if j < LAG and before is not None:
                        for last in (((0, 1), (2,), ()) if slots > NT else ((0,), (1,), (2,)))[j]:
                            down(*before, NT - LAG + last)
                    if LAG <= j < NT + LAG:
                        down(*main, j - LAG)
                    if j == steps.get("mixer out"):
                        pe.wait_ge(*free["mixer out"])
                        pe.wait_ge(y_lo_done, chain + 1)
                        mixer_out(chain)
                    if j == steps.get("transpose ffn 4"):
                        pe.wait_ge(*free["transpose ffn 4"])
                        transpose_ffn(4, output)
                    if j == steps.get("transpose 4"):
                        pe.wait_ge(*free["transpose 4"])
                        transpose_norm(4, tail)
                    if j == steps.get("router 4"):
                        router(4, tail)
                    if j == steps.get("transpose 1"):
                        pe.wait_ge(*free["transpose 1"])
                        transpose_norm(1, prepare)
                    if j == steps.get("router 1"):
                        router(1, prepare)
                    if j == steps.get("transpose ffn 1"):
                        pe.wait_ge(*free["transpose ffn 1"])
                        transpose_ffn(1, chain)
                    if j == steps.get("transpose 2"):
                        pe.wait_ge(ffn_added[1], chain + 1)
                        transpose_norm(2, chain)
                    if j == steps.get("mixer gate"):
                        pe.wait_ge(xT_lo_done[2], chain + 1)
                        product(side[:, :], wt_hi[:, WIN_G, :], xT_hi[2][:, :], xT_lo[2][:, :], wt_lo[:, WIN_G, :],
                                True, True).then_inc(mix_gate_ready, 1)
                    if j == steps.get("mixer value"):
                        pe.wait_ge(mix_gate_done, chain + 1)
                        product(side[:, :], wt_hi[:, WIN_V, :], xT_hi[2][:, :], xT_lo[2][:, :], wt_lo[:, WIN_V, :],
                                True, True).then_inc(mix_val_ready, 1)

            def free_first(i):
                return {"weights": (res_done, i), "transpose ffn 4": (wT_done[1], i + 1),
                        "transpose 4": (halved_done, i - 1)}

            def free_second(i):
                return {"mixer out": (mix_val_done, i + 1), "transpose 1": (wT_done[4], i),
                        "transpose ffn 1": (route[1], (i + 1) * ROUTE + LOGITS_READ)}

            pe.wait_ge(pool_const, 4)
            weights(0)
            weights(1)
            transpose_norm(1, 0)
            weights(2)
            pe.wait_ge(w_lo_done, 1)
            router(1, 0)
            weights(3)
            for n in range(4, NBATCH):
                weights(n)
            pe.wait_ge(pool_const, 7)
            pe.wait_ge(w_lo_done, NBATCH)
            unit((1, 0), FIRST, {"transpose 1": (wT_done[1], 1)}, prepare=1)
            unit((1, 1), {**BOTH, **AFTER_BOTH}, {"transpose ffn 1": (wT_done[1], 2), "mixer out": (mix_val_done, 1),
                                "transpose 4": (res_done, 1)},
                 before=(1, 0), chain=0, tail=0, prepare=2, slots=BOTH_SLOTS)
            unit((4, 0), {**CHAIN, **PREPARE}, free_second(1), chain=1, prepare=2)
            with pe.Fori(2, NBLK - 1) as i:
                unit((1, i), {**TAIL, **OUTPUT, **NEXT}, free_first(i), before=(4, i - 2), output=i - 2,
                     tail=i - 1, prepare=i + 1)
                unit((4, i - 1), {**CHAIN, **PREPARE}, free_second(i), before=(1, i), chain=i, prepare=i + 1)
            unit((1, NBLK - 1), {**TAIL, **OUTPUT}, free_first(NBLK - 1), before=(4, NBLK - 3), output=NBLK - 3,
                 tail=NBLK - 2)
            unit((4, NBLK - 2), BOTH, {"transpose ffn 1": (wT_done[4], NBLK - 1), "mixer out": (mix_val_done, NBLK),
                                       "transpose 4": (res_done, NBLK)},
                 before=(1, NBLK - 1), chain=NBLK - 1, tail=NBLK - 1, slots=BOTH_SLOTS)
            unit((4, NBLK - 1), {**OUTPUT, "keep x2": 9}, {"transpose ffn 4": (wT_done[4], NBLK)},
                 output=NBLK - 2, tail=NBLK - 1, slots=NT + LAG)
            pe.wait_ge(halved_done, NBLK - 1)
            transpose_ffn(4, NBLK - 1)


_INS = ["L0_attn_x", "L0_attn_W_in", "L0_attn_conv_w", "L0_attn_conv_b", "L0_attn_a_param", "L0_attn_W_out",
        "L0_attn_ln_w", "L0_attn_ln_b", "L0_ffn_router_weight", "L0_ffn_router_bias", "L0_ffn_gate_w",
        "L0_ffn_up_w", "L0_ffn_down_w", "L0_ffn_shared_gate_w", "L0_ffn_shared_up_w", "L0_ffn_shared_down_w"]


def kernel(**inputs):
    import numpy as np
    import concourse.bacc as bacc
    from concourse.bass_utils import run_bass_kernel_spmd

    nc = bacc.Bacc("TRN2", target_bir_lowering=False, num_devices=1)
    arrays, args = {}, []
    for name in _INS:
        a = np.ascontiguousarray(inputs[name])
        arrays[f"in_{name}"] = a
        args.append(nc.dram_tensor(f"in_{name}", a.shape, mybir.dt.from_np(a.dtype), kind="ExternalInput").ap())
    shape = arrays["in_L0_attn_x"].shape
    out = nc.dram_tensor("out_x", shape, F32, kind="ExternalOutput").ap()
    macaron_kernel(nc, *args, out)
    r = run_bass_kernel_spmd(nc, [arrays], core_ids=[0])
    return r.results[0]["out_x"]
```
